# Optimizing a Trainium2 kernel written in Bass

```python
import numpy as np
import jax
import jax.numpy as jnp

def _softmax(x, axis=-1):
    return jax.nn.softmax(x, axis=axis)

def _gelu(x):
    return jax.nn.gelu(x, approximate=True)

def _silu(x):
    return jax.nn.silu(x)

def _sigmoid(x):
    return jax.nn.sigmoid(x)

def _layernorm(x, axis=-1, eps=1e-05):
    m = jnp.mean(x, axis=axis, keepdims=True)
    v = jnp.var(x, axis=axis, keepdims=True)
    return (x - m) / jnp.sqrt(v + eps)

def _scatter_add(tgt, idx, src, axis=0):
    return tgt.at[idx].add(src)

def _segment_sum(src, seg, n):
    return jax.ops.segment_sum(src, seg, n)
kernel_name = 'mk_adj_resnorm_d4_adj_r2_dbf070'

def setup_inputs(seed: int=0):
    np.random.seed(seed)
    _w = jnp.asarray

    def _rec_inputs():
        import jax
        import jax.numpy as jnp
        _gk = jax.random.key(seed)
        x = -0.0001117 + 0.9999 * jax.random.normal(jax.random.fold_in(_gk, 1), (16, 512, 256), jnp.float32)
        _a = jax.random.bernoulli(jax.random.fold_in(_gk, 2), 0.00390625, (512, 512))
        _a = jnp.logical_or(_a, jnp.swapaxes(_a, -1, -2))
        _a = jnp.logical_or(_a, jnp.eye(512, dtype=bool))
        adj = _a.astype(jnp.int32)
        return (x, adj)
    x, adj = _rec_inputs()

    def _L0_gnn_setup():
        import jax, jax.numpy as jnp
        import numpy as np
        B, N, F, F1 = (512, 75, 256, 128)
        NEG = -1000000000.0
        ALPHA = 0.2
        key = jax.random.key(seed)
        k1, k2, k3, k4 = jax.random.split(key, 4)
        X = jax.random.normal(k1, (B, N, F), dtype=jnp.float32)
        A = jax.random.randint(k2, (N, N), 0, 2, dtype=jnp.int32)
        W = jax.random.normal(k3, (F, F1), dtype=jnp.float32) * (1.0 / np.sqrt(F))
        a = jax.random.normal(k4, (2, F1, 1), dtype=jnp.float32) * (1.0 / np.sqrt(F1))
        return {'X': X, 'A': A, 'W': W, 'a': a}
    _L0_gnn_all = _L0_gnn_setup()
    _L0_gnn_in = {k: v for k, v in _L0_gnn_all.items() if k in ('W', 'a')}
    del _L0_gnn_all

    def _L1_gnn_setup():
        import jax, jax.numpy as jnp
        import numpy as np
        D_MODEL = 256
        NUM_HEADS = 8
        D_HEAD = D_MODEL // NUM_HEADS
        B, N = (4, 1024)
        key = jax.random.key(seed)
        ks = jax.random.split(key, 10)
        s = 1.0 / np.sqrt(D_MODEL)
        inp = {'h': jax.random.normal(ks[0], (B, N, D_MODEL), dtype=jnp.float32), 'adj': jax.random.randint(ks[1], (N, N), 0, 2, dtype=jnp.int32), 'Wq': jax.random.uniform(ks[2], (D_MODEL, D_MODEL), jnp.float32, -s, s), 'bq': jax.random.uniform(ks[3], (D_MODEL,), jnp.float32, -s, s), 'Wk': jax.random.uniform(ks[4], (D_MODEL, D_MODEL), jnp.float32, -s, s), 'bk': jax.random.uniform(ks[5], (D_MODEL,), jnp.float32, -s, s), 'Wv': jax.random.uniform(ks[6], (D_MODEL, D_MODEL), jnp.float32, -s, s), 'bv': jax.random.uniform(ks[7], (D_MODEL,), jnp.float32, -s, s), 'Wo': jax.random.uniform(ks[8], (D_MODEL, D_MODEL), jnp.float32, -s, s), 'bo': jax.random.uniform(ks[9], (D_MODEL,), jnp.float32, -s, s)}
        return inp
    _L1_gnn_all = _L1_gnn_setup()
    _L1_gnn_in = {k: v for k, v in _L1_gnn_all.items() if k in ('Wq', 'bq', 'Wk', 'bk', 'Wv', 'bv', 'Wo', 'bo')}
    del _L1_gnn_all

    def _L2_gnn_setup():
        import jax, jax.numpy as jnp
        import numpy as np
        B, N, D = (8, 1024, 256)
        NEG_SLOPE = 0.2
        key = jax.random.key(seed)
        k1, k2, k3, k4, k5 = jax.random.split(key, 5)
        x = jax.random.normal(k1, (B, N, D), dtype=jnp.float32)
        adj = jax.random.randint(k2, (N, N), 0, 2, dtype=jnp.int32)
        adj = jnp.maximum(adj, jnp.eye(N, dtype=jnp.int32))
        W = jax.random.normal(k3, (D, D), dtype=jnp.float32) * (1.0 / np.sqrt(D))
        a_src = jax.random.normal(k4, (D,), dtype=jnp.float32) * (1.0 / np.sqrt(D))
        a_dst = jax.random.normal(k5, (D,), dtype=jnp.float32) * (1.0 / np.sqrt(D))
        return {'x': x, 'adj': adj, 'W': W, 'a_src': a_src, 'a_dst': a_dst}
    _L2_gnn_all = _L2_gnn_setup()
    _L2_gnn_in = {k: v for k, v in _L2_gnn_all.items() if k in ('W', 'a_src', 'a_dst')}
    del _L2_gnn_all

    def _L3_gnn_setup():
        import jax, jax.numpy as jnp
        import numpy as np
        LEAKY_ALPHA = 0.01
        NEG_INF = -1000000000.0
        LN_EPS = 1e-05

        def _gat_heads(x, adj, W, a):
            O = W.shape[-1]
            Wh = jnp.einsum('bnf,hfo->bhno', x, W)
            f1 = jnp.einsum('bhno,ho->bhn', Wh, a[:, :O])
            f2 = jnp.einsum('bhno,ho->bhn', Wh, a[:, O:])
            e = f1[:, :, :, None] + f2[:, :, None, :]
            e = jnp.where(e > 0, e, LEAKY_ALPHA * e)
            e = jnp.where(adj[None, None] > 0, e, NEG_INF)
            attn = jax.nn.softmax(e, axis=-1)
            return jnp.einsum('bhnm,bhmo->bhno', attn, Wh)
        key = jax.random.key(seed)
        ks = jax.random.split(key, 10)
        B, N, F_in, F_hid, H, F_out, D_ff = (8, 1024, 256, 256, 4, 256, 256)
        s = 0.05
        return {'enc_inputs': jax.random.normal(ks[0], (B, N, F_in), jnp.float32), 'adj': jax.random.randint(ks[1], (N, N), 0, 2, jnp.int32), 'W_heads': jax.random.normal(ks[2], (H, F_in, F_hid), jnp.float32) * s, 'a_heads': jax.random.normal(ks[3], (H, 2 * F_hid), jnp.float32) * s, 'W_out': jax.random.normal(ks[4], (H * F_hid, F_out), jnp.float32) * s, 'a_out': jax.random.normal(ks[5], (2 * F_out,), jnp.float32) * s, 'w1': jax.random.normal(ks[6], (F_out, D_ff), jnp.float32) * s, 'b1': jnp.zeros((D_ff,), jnp.float32), 'w2': jax.random.normal(ks[7], (D_ff, F_out), jnp.float32) * s, 'b2': jnp.zeros((F_out,), jnp.float32), 'ln_gamma': jnp.ones((F_out,), jnp.float32), 'ln_beta': jnp.zeros((F_out,), jnp.float32)}
    _L3_gnn_all = _L3_gnn_setup()
    _L3_gnn_in = {k: v for k, v in _L3_gnn_all.items() if k in ('W_heads', 'a_heads', 'W_out', 'a_out', 'w1', 'b1', 'w2', 'b2', 'ln_gamma', 'ln_beta')}
    del _L3_gnn_all
    return {'x': x, 'adj': adj, 'L0_gnn_W': _L0_gnn_in['W'], 'L0_gnn_a': _L0_gnn_in['a'], 'L1_gnn_Wq': _L1_gnn_in['Wq'], 'L1_gnn_bq': _L1_gnn_in['bq'], 'L1_gnn_Wk': _L1_gnn_in['Wk'], 'L1_gnn_bk': _L1_gnn_in['bk'], 'L1_gnn_Wv': _L1_gnn_in['Wv'], 'L1_gnn_bv': _L1_gnn_in['bv'], 'L1_gnn_Wo': _L1_gnn_in['Wo'], 'L1_gnn_bo': _L1_gnn_in['bo'], 'L2_gnn_W': _L2_gnn_in['W'], 'L2_gnn_a_src': _L2_gnn_in['a_src'], 'L2_gnn_a_dst': _L2_gnn_in['a_dst'], 'L3_gnn_W_heads': _L3_gnn_in['W_heads'], 'L3_gnn_a_heads': _L3_gnn_in['a_heads'], 'L3_gnn_W_out': _L3_gnn_in['W_out'], 'L3_gnn_a_out': _L3_gnn_in['a_out'], 'L3_gnn_w1': _L3_gnn_in['w1'], 'L3_gnn_b1': _L3_gnn_in['b1'], 'L3_gnn_w2': _L3_gnn_in['w2'], 'L3_gnn_b2': _L3_gnn_in['b2'], 'L3_gnn_ln_gamma': _L3_gnn_in['ln_gamma'], 'L3_gnn_ln_beta': _L3_gnn_in['ln_beta']}

def reference(x, adj, L0_gnn_W, L0_gnn_a, L1_gnn_Wq, L1_gnn_bq, L1_gnn_Wk, L1_gnn_bk, L1_gnn_Wv, L1_gnn_bv, L1_gnn_Wo, L1_gnn_bo, L2_gnn_W, L2_gnn_a_src, L2_gnn_a_dst, L3_gnn_W_heads, L3_gnn_a_heads, L3_gnn_W_out, L3_gnn_a_out, L3_gnn_w1, L3_gnn_b1, L3_gnn_w2, L3_gnn_b2, L3_gnn_ln_gamma, L3_gnn_ln_beta):
    import jax
    import jax.numpy as jnp

    def _L0_gnn_ref(X, A, W, a):
        import jax, jax.numpy as jnp
        import numpy as np
        B, N, F, F1 = (512, 75, 256, 128)
        NEG = -1000000000.0
        ALPHA = 0.2
        h = jnp.einsum('bnf,fo->bno', X, W)
        att_self = jnp.einsum('bno,od->bnd', h, a[0])
        att_neigh = jnp.einsum('bno,od->bnd', h, a[1])
        e = att_self + jnp.swapaxes(att_neigh, 1, 2)
        e = jax.nn.leaky_relu(e, ALPHA)
        adj = A.astype(h.dtype)
        e = e + NEG * (1.0 - adj)[None, :, :]
        alpha = jax.nn.softmax(e, axis=-1)
        out = jnp.einsum('bij,bjo->bio', alpha, h)
        return jnp.concatenate([out, h], axis=-1)

    def _L1_gnn_ref(h, adj, Wq, bq, Wk, bk, Wv, bv, Wo, bo):
        import jax, jax.numpy as jnp
        import numpy as np
        D_MODEL = 256
        NUM_HEADS = 8
        D_HEAD = D_MODEL // NUM_HEADS
        B, N = (4, 1024)
        b, n, _ = h.shape

        def split_heads(x):
            return x.reshape(b, n, NUM_HEADS, D_HEAD).transpose(0, 2, 1, 3)
        q = split_heads(h @ Wq.T + bq)
        k = split_heads(h @ Wk.T + bk)
        v = split_heads(h @ Wv.T + bv)
        scale = 1.0 / np.sqrt(D_HEAD)
        scores = jnp.einsum('bhqd,bhkd->bhqk', q, k) * scale
        mask = (adj == 0)[None, None, :, :]
        scores = jnp.where(mask, -jnp.inf, scores)
        attn = jax.nn.softmax(scores, axis=-1)
        out = jnp.einsum('bhqk,bhkd->bhqd', attn, v)
        out = out.transpose(0, 2, 1, 3).reshape(b, n, D_MODEL)
        return out @ Wo.T + bo

    def _L2_gnn_ref(x, adj, W, a_src, a_dst):
        import jax, jax.numpy as jnp
        import numpy as np
        B, N, D = (8, 1024, 256)
        NEG_SLOPE = 0.2
        Wh = jnp.einsum('bnd,de->bne', x, W)
        e_src = jnp.einsum('bnd,d->bn', Wh, a_src)
        e_dst = jnp.einsum('bnd,d->bn', Wh, a_dst)
        logits = e_src[:, :, None] + e_dst[:, None, :]
        logits = jnp.where(logits >= 0, logits, NEG_SLOPE * logits)
        mask = (adj == 0)[None, :, :]
        logits = jnp.where(mask, -jnp.inf, logits)
        attn = jax.nn.softmax(logits, axis=-1)
        attn = jnp.nan_to_num(attn, nan=0.0)
        out = jnp.einsum('bnm,bmd->bnd', attn, Wh)
        return out

    def _L3_gnn_ref(enc_inputs, adj, W_heads, a_heads, W_out, a_out, w1, b1, w2, b2, ln_gamma, ln_beta):
        import jax, jax.numpy as jnp
        import numpy as np
        LEAKY_ALPHA = 0.01
        NEG_INF = -1000000000.0
        LN_EPS = 1e-05

        def _gat_heads(x, adj, W, a):
            O = W.shape[-1]
            Wh = jnp.einsum('bnf,hfo->bhno', x, W)
            f1 = jnp.einsum('bhno,ho->bhn', Wh, a[:, :O])
            f2 = jnp.einsum('bhno,ho->bhn', Wh, a[:, O:])
            e = f1[:, :, :, None] + f2[:, :, None, :]
            e = jnp.where(e > 0, e, LEAKY_ALPHA * e)
            e = jnp.where(adj[None, None] > 0, e, NEG_INF)
            attn = jax.nn.softmax(e, axis=-1)
            return jnp.einsum('bhnm,bhmo->bhno', attn, Wh)
        B, N, _ = enc_inputs.shape
        h = jax.nn.elu(_gat_heads(enc_inputs, adj, W_heads, a_heads))
        h = jnp.transpose(h, (0, 2, 1, 3)).reshape(B, N, -1)
        out = _gat_heads(h, adj, W_out[None], a_out[None])[:, 0]
        out = jax.nn.elu(out)
        ffn = jnp.maximum(out @ w1 + b1, 0.0) @ w2 + b2
        y = ffn + out
        mu = jnp.mean(y, axis=-1, keepdims=True)
        var = jnp.var(y, axis=-1, keepdims=True)
        return (y - mu) / jnp.sqrt(var + LN_EPS) * ln_gamma + ln_beta
    x = _layernorm(x + _L0_gnn_ref(x, adj, L0_gnn_W, L0_gnn_a), axis=-1)
    x = _layernorm(x + _L1_gnn_ref(x, adj, L1_gnn_Wq, L1_gnn_bq, L1_gnn_Wk, L1_gnn_bk, L1_gnn_Wv, L1_gnn_bv, L1_gnn_Wo, L1_gnn_bo), axis=-1)
    x = _layernorm(x + _L2_gnn_ref(x, adj, L2_gnn_W, L2_gnn_a_src, L2_gnn_a_dst), axis=-1)
    x = _layernorm(x + _L3_gnn_ref(x, adj, L3_gnn_W_heads, L3_gnn_a_heads, L3_gnn_W_out, L3_gnn_a_out, L3_gnn_w1, L3_gnn_b1, L3_gnn_w2, L3_gnn_b2, L3_gnn_ln_gamma, L3_gnn_ln_beta), axis=-1)
    return x

_drawn_inputs = setup_inputs


def setup_inputs(seed=0):
    import zlib

    import numpy as np

    out = dict(_drawn_inputs(seed))
    spreads = {'L3_gnn_b1': (0.0, 0.1),
     'L3_gnn_b2': (0.0, 0.1),
     'L3_gnn_ln_gamma': (1.0, 0.2),
     'L3_gnn_ln_beta': (0.0, 0.1)}
    factors = {'L1_gnn_bq': 8.0, 'L1_gnn_bk': 8.0}
    for name, (base, spread) in spreads.items():
        noise = np.random.default_rng([zlib.crc32(name.encode()), seed]).standard_normal(out[name].shape)
        drawn = base * np.exp(spread * noise) if base else spread * noise
        out[name] = jnp.asarray(drawn.astype(out[name].dtype))
    for name, factor in factors.items():
        out[name] = (out[name] * factor).astype(out[name].dtype)
    return out
```

```python
from contextlib import ExitStack

import concourse.bass as bass
from concourse import mybir

F32 = mybir.dt.float32
F32R = mybir.dt.float32r
BF16 = mybir.dt.bfloat16
I32 = mybir.dt.int32
ALU = mybir.AluOpType
ACT = mybir.ActivationFunctionType

P = 128
B, N, D = 16, 512, 256
T = N // P
K = D // P
O0 = D // 2
H1 = 8
DH = D // H1
H3 = 4
BANK = 512
RING = 3
FAR = float(2 ** 60)
EPS = 1e-5
SCALE = float(DH) ** -0.5
SLOPE = {"L0": 0.2, "L2": 0.2, "L3": 0.01}

F_HEADS, B_HEADS = H1 + 2, H3 + 1


def front_stages():
    s = [("xpose", 0), ("fcols", 0), ("bias", 0), ("fbc", 0), ("wh", 0), ("addh", 0), ("exp", 0),
         ("ptrans", 0), ("attn", 0), ("norm", 0),
         ("xbo", 1), ("xpose", 1), ("qk", 1), ("v", 1), ("scores", 1), ("scores", 2)]
    for h in range(1, H1 + 1):
        s += [("exp", h), ("ptrans", h)]
        s += [("scores", h + 2)] if h + 2 <= H1 else []
        s += [("attn", h)]
    s += [("zbc", 1), ("oproj", 1), ("norm", 1),
          ("xpose", 2), ("fcols", 9), ("bias", 9), ("fbc", 9), ("wh", 9), ("exp", 9),
          ("ptrans", 9), ("attn", 9), ("norm", 2)]
    return s


def back_stages():
    s = [("xbeta", 0), ("xpose", 0), ("fcols", 0), ("bias", 0), ("fbc", 0), ("wh", 0),
         ("bias", 1), ("fbc", 1), ("wh", 1)]
    for h in range(H3):
        s += [("exp", h), ("ptrans", h)]
        s += [("bias", h + 2), ("fbc", h + 2)] if h + 2 < H3 else []
        s += [("zbc", h), ("attn", h)]
        s += [("wh", h + 2)] if h + 2 < H3 else []
    s += [("wh", 4), ("fcols", 4), ("bias", 4), ("fbc", 4), ("exp", 4), ("ptrans", 4), ("attn", 4),
          ("xpose", 4), ("w1", 4), ("w2", 4), ("norm", 3), ("affine", 3), ("norm", 4), ("store", 4)]
    return s


def banks(half, stage, h):
    if stage in ("scores", "ptrans"):
        return T
    if stage in ("fcols", "fbc"):
        return 1
    if stage == "wh":
        return 1 if (half, h) == ("f", 0) else 2
    if stage == "attn":
        return (1 if h == 0 else 2 if h == 9 else 0) if half == "f" else 2
    if stage == "zbc":
        return 2 if half == "f" else 1
    return {"xpose": 2, "qk": 4, "v": 2, "oproj": 2, "w1": 2, "w2": 2}.get(stage, 0)


STAGES = {"f": front_stages(), "b": back_stages()}

TURNS = {
    "sp": (
        2, 1),
    "pe": (
        2, 2, 2, 1, 1, 11, 5, 5, 2, 2, 1, 3, 2, 1, 1, 6, 1, 2, 3, 2, 2, 1, 6, 1, 2, 1, 1, 1, 9, 1, 8, 1, 2,
        2, 16, 1, 1, 1, 4, 2, 21, 2, 1, 2, 1, 2, 5, 2, 1, 4, 6),
    "act": (
        1, 1, 1, 1, 1, 8, 7, 6, 1, 4, 1, 1, 2, 1, 1, 10, 4, 2, 1, 2, 6, 2, 6, 1, 1, 1, 4, 2, 12, 2, 14, 1,
        2, 6, 1, 1, 2, 3, 7),
    "pool": (
        0, 9, 5, 4, 2, 8, 3, 1, 2, 3, 1),
    "dve": (
        1, 8, 1, 1, 3, 4, 2, 1, 1, 2, 1, 2, 6, 3, 1, 2, 1, 1, 1, 1, 2, 8, 1, 2, 3, 1, 3, 1, 4, 1, 3, 1, 8,
        1, 3, 1, 5, 2, 2, 1, 7, 1, 4, 1, 10, 1, 3, 2, 3, 1, 3, 2, 4, 1, 4, 1, 1, 3, 5, 5, 2, 4, 1, 2, 1, 1,
        1, 1, 2, 3, 4, 1),
}


def take_turns(engine, front, back):
    for n, count in enumerate(TURNS[engine]):
        for _ in range(count):
            next((front, back)[n % 2], None)
    for half in (front, back):
        assert next(half, half) is half


def first_jobs(half, stages):
    at, first = 0, {}
    for s, h in stages:
        if banks(half, s, h):
            first[s, h] = at
            at += banks(half, s, h)
    return first, at


class Count:

    def __init__(self, sem, per_graph):
        self.sem, self.per_graph = sem, per_graph

    def at(self, b, n):
        return b * self.per_graph + n


class Ring:

    def __init__(self, ctx, nc, half, stages):
        self.first, self.jobs = first_jobs(half, stages)
        self.bank = [ctx.enter_context(nc.psum_tensor(f"{half}_ring{k}", [P, BANK], F32)) for k in range(RING)]
        self.uses = [(self.jobs - k + RING - 1) // RING for k in range(RING)]
        self.full = [ctx.enter_context(nc.semaphore(f"{half}_full{k}")) for k in range(RING)]
        self.drained = [ctx.enter_context(nc.semaphore(f"{half}_drained{k}")) for k in range(RING)]

    def job(self, stage, h, n=0):
        return self.first[stage, h] + n

    def ps(self, job):
        return self.bank[job % RING]

    def count(self, b, job):
        return b * self.uses[job % RING] + job // RING + 1


def graph_layers(nc, x, adj, w, out):
    ctx = ExitStack()
    with ctx:
        def sb(name, shape, dt=F32):
            return ctx.enter_context(nc.sbuf_tensor(name, shape, dt))

        def sem(name):
            return ctx.enter_context(nc.semaphore(name))

        fr = Ring(ctx, nc, "f", STAGES["f"])
        bk = Ring(ctx, nc, "b", STAGES["b"])
        ring = {"f": fr, "b": bk}
        heads_out = [ctx.enter_context(nc.psum_tensor(f"heads_out{k}", [P, BANK], F32)) for k in range(K)]

        W0 = sb("W0", [P, K, O0])
        WQ, WK, WV, WO = (sb(n, [P, K, D]) for n in ("WQ", "WK", "WV", "WO"))
        W2 = sb("W2", [P, K, D])
        W3 = sb("W3", [P, K, H3, D])
        W4 = sb("W4", [P, H3 * K, D])
        FF1, FF2 = sb("FF1", [P, K, D]), sb("FF2", [P, K, D])
        WA = sb("WA", [P, 40])
        A0, A2, A3, A4 = sb("A0", [P, 2]), sb("A2", [P, K, 2]), sb("A3", [P, K, H3, 2]), sb("A4", [P, K, 2])
        BQK, B1 = sb("BQK", [P, 2, K]), sb("B1", [P, K])
        BV, BO, B2, GAMMA, BETA = (sb(n, [P, D]) for n in ("BV", "BO", "B2", "GAMMA", "BETA"))
        mask = sb("mask", [P, T, N], BF16)
        ident = sb("ident", [P, P])
        minus_half = sb("minus_half", [P, T])

        x_in = sb("x_in", [P, T, D])
        xf, yf = sb("xf", [P, T, D]), sb("yf", [P, T, D])
        xtf = sb("xtf", [P, K, N])
        whf = sb("whf", [P, T, D])
        ptf = sb("ptf", [P, 2, T, N])
        parts = ptf
        stack = sb("stack", [P, K, 2, H1 // K, N], F32R)
        rzbf = sb("rzbf", [P, K, N])
        xb, yb, ob = sb("xb", [P, T, D]), sb("yb", [P, T, D]), sb("ob", [P, T, D])
        xtb = sb("xtb", [P, K, N])
        whb = sb("whb", [P, 2, T, D])
        ptb = sb("ptb", [P, T, N])
        rzbb = sb("rzbb", [P, N])
        ht = sb("ht", [P, H3 * K, N])
        pre, ex = sb("pre", [P, K * N]), sb("ex", [P, K * N])
        Z = {h: sb(f"Z{h}", [P, 2, T, N]) for h in "fb"}
        FC = {h: sb(f"FC{h}", [P, T, 8]) for h in "fb"}
        G = {h: sb(f"G{h}", [P, 2, T]) for h in "fb"}
        NG = {h: sb(f"NG{h}", [P, 2, T]) for h in "fb"}
        NM = {h: sb(f"NM{h}", [P, 2, T]) for h in "fb"}
        ZS = {h: sb(f"ZS{h}", [P, 2, T]) for h in "fb"}
        RZ = {h: sb(f"RZ{h}", [P, 2, T]) for h in "fb"}
        zs1 = sb("zs1", [P, T, H1])
        rz1 = xtf[:, :, :].rearrange("p k (a d) -> p (k a) d", a=K)
        ST = {h: sb(f"ST{h}", [P, T, 6]) for h in "fb"}
        MV = {h: sb(f"MV{h}", [P, T, 2]) for h in "fb"}
        VE = {h: sb(f"VE{h}", [P, T]) for h in "fb"}
        RS = {h: sb(f"RS{h}", [P, T]) for h in "fb"}

        s_w = sem("weights_loaded")
        s_adj = sem("adjacency_loaded")
        s_id = sem("constants_made")
        s_wa = sem("attention_weights")
        s_mask = sem("mask_made")
        x_loaded = Count(sem("x_loaded"), 16)
        stacked = [Count(sem(f"stacked{r}"), 4 * 16) for r in range(4)]
        stored = Count(sem("stored"), 16)
        biased = {"f": Count(sem("f_biased"), 2 * T), "b": Count(sem("b_biased"), B_HEADS * T)}
        logits = {"f": Count(sem("f_logits"), 3 + H1 + 3), "b": Count(sem("b_logits"), 3 * B_HEADS)}
        probs = {"f": Count(sem("f_probs"), F_HEADS * T), "b": Count(sem("b_probs"), B_HEADS * T)}
        recips = {"f": Count(sem("f_recips"), 3), "b": Count(sem("b_recips"), B_HEADS)}
        stats = {"f": Count(sem("f_stats"), 3 * 3), "b": Count(sem("b_stats"), 3 * 2)}
        rstd = {"f": Count(sem("f_rstd"), 3), "b": Count(sem("b_rstd"), 2)}
        normed = {"f": Count(sem("f_normed"), 3 * T), "b": Count(sem("b_normed"), 2 * T)}
        added = {"f": Count(sem("f_added"), 2), "b": Count(sem("b_added"), 3)}
        high_part = Count(sem("high_part"), 4)
        heads_done = Count(sem("heads_done"), H1)
        o_ready = Count(sem("o_ready"), K)
        ex_done = Count(sem("ex_done"), B_HEADS)
        elu_low = Count(sem("elu_low"), B_HEADS)
        elu_done = Count(sem("elu_done"), B_HEADS)
        summed = Count(sem("summed"), 1)

        def logit_steps(half, h):
            if half == "b":
                return 3 * h
            return 0 if h == 0 else 3 + (h - 1)

        def zbuf(half, h):
            return Z[half][:, h % 2]

        def pt(half, h):
            return ptf[:, h % 2] if half == "f" else ptb[:, :, :]

        def last_user(half, h):
            return (0, h - 2) if h >= 2 else (-1, F_HEADS - 2 + h)

        def additive(half, h):
            return half == "b" or h in (0, 9)

        def turned_by_vector(half, h, t):
            return t == 3 if additive(half, h) else t % 2 == 1

        def slope(half, h):
            return SLOPE["L3"] if half == "b" else SLOPE["L0"]

        def wa_of(half, h):
            if half == "f":
                return WA[:, 0:4].rearrange("p (k c) -> p k c", k=K) if h == 0 else \
                    WA[:, 4:8].rearrange("p (k c) -> p k c", k=K)
            return WA[:, 8:24].rearrange("p (k c) -> p k c", k=K) if h == 0 else \
                WA[:, 24:40].rearrange("p (k c) -> p k c", k=H3 * K)

        def fcol(half, h, which):
            c = 2 * h if half == "b" and h < H3 else 0
            return FC[half][:, :, c + which:c + which + 1]

        def ahead(eng, value):
            if not isinstance(value, int):
                eng.lower_val(value)
            return value

        def later(b):
            return not (isinstance(b, int) and b == 0)

        block = ctx.enter_context(nc.Block())

        @block.sync
        def _(sp):
            zf = Z["f"][:, :, :, :].rearrange("p a t n -> p (a t n)")
            zb = Z["b"][:, :, :, :].rearrange("p a t n -> p (a t n)")
            sp.dma_start(x_in[:, :, :], x[0]).then_inc(x_loaded.sem, 16)
            sp.dma_start(zb[:, 0:T * N].bitcast(I32), adj).then_inc(s_adj, 16)
            loads = [(A0, "a0"), (A2, "a2"), (A3, "a3"), (A4, "a4"), (zf[:, 0:256], "w0t"), (zf[:, 256:768], "w2t"),
                     (zf[:, T * N:2 * T * N], "w3t"), (zb[:, T * N:2 * T * N], "w4t"),
                     (W0, "w0"), (BQK, "bqk"), (WQ, "wq"), (WK, "wk"), (WV, "wv"), (BV, "bv"), (WO, "wo"), (BO, "bo"),
                     (W2, "w2"), (W3, "w3"), (W4, "w4"), (FF1, "f1"), (B1, "b1"), (FF2, "f2"), (B2, "b2"),
                     (GAMMA, "gamma"), (BETA, "beta")]
            assert len(loads) == N_LOADS
            for dst, name in loads:
                dst = dst[(slice(None),) * len(dst.shape)]
                sp.dma_start(dst, w[name]).then_inc(s_w, 16)

            def one(a, b):
                return a[bass.ds(b, 1)].rearrange("o p t d -> (o p) t d")

            def steps(half, b):
                for stage, h in STAGES[half] if b is not None else ():
                    if (half, stage) == ("f", "v"):
                        sent = fr.job("qk", 1, 3)
                        seen = ahead(sp, fr.count(b, sent))
                        sp.wait_ge(s_adj, 16)
                        sp.wait_ge(fr.drained[sent % RING], seen)
                        for r in range(4):
                            rows = slice(DH * r, DH * (r + 1))
                            done = stacked[r].sem
                            for q in range(2):
                                sp.dma_start(stack[0:DH, :, q, r, :].bitcast(F32),
                                             parts[rows, :, 1 + q]).then_inc(done, 16)
                            for g, first in ((1, 1), (2, 0)):
                                src = parts[rows].rearrange("p m (a c) n -> p c (m a) n", c=2)
                                sp.dma_start(stack[DH * g:DH * (g + 1), :, :, r, :]
                                             .rearrange("p m q n -> p (m q) n").bitcast(F32),
                                             src[:, first]).then_inc(done, 16)
                        yield
                    if (half, stage, h) == ("f", "norm", 0) and not (isinstance(b, int) and b == B - 1):
                        seen = ahead(sp, normed["f"].at(b, T))
                        sp.wait_ge(s_adj, 16)
                        sp.wait_ge(normed["f"].sem, seen)
                        src = x[b + 1] if isinstance(b, int) else one(x, b + 1)
                        sp.dma_start(x_in[:, :, :], src).then_inc(x_loaded.sem, 16)
                        yield
                    if (half, stage) == ("b", "store"):
                        seen = ahead(sp, normed["b"].at(b, 2 * T))
                        sp.wait_ge(s_adj, 16)
                        sp.wait_ge(normed["b"].sem, seen)
                        dst = out[b] if isinstance(b, int) else one(out, b)
                        sp.dma_start(dst, ob[:, :, :]).then_inc(stored.sem, 16)
                        yield

            def program(b_front, b_back):
                take_turns("sp", steps("f", b_front), steps("b", b_back))

            program(0, None)
            program(1, 0)
            with sp.Fori(1, B - 2) as t:
                program(t + 1, t)
            program(B - 1, B - 2)
            program(None, B - 1)
            sp.wait_ge(stored.sem, stored.at(B - 1, 16))

        @block.tensor
        def _(pe):
            pe.wait_ge(s_w, 16 * N_LOADS)
            pe.wait_ge(s_id, 3)
            zf = Z["f"][:, :, :, :].rearrange("p a t n -> p (a t n)")
            zb = Z["b"][:, :, :, :].rearrange("p a t n -> p (a t n)")
            w0t, w2t = zf[:, 0:256], zf[:, 256:768].rearrange("p (o f) -> p o f", o=K)
            w3t = zf[:, T * N:2 * T * N].rearrange("p (h o f) -> p h o f", h=H3, o=K)
            w4t = zb[:, T * N:2 * T * N].rearrange("p (o f) -> p o f", o=K)
            wa = heads_out[0]
            for k in range(K):
                fs = slice(k * P, (k + 1) * P)
                pe.matmul(wa[:, 2 * k:2 * k + 2], w0t[:, fs], A0[:, :], start=True, stop=True)
                for o in range(K):
                    pe.matmul(wa[:, 4 + 2 * k:6 + 2 * k], w2t[:, o, fs], A2[:, o, :], start=o == 0, stop=o == K - 1)
                for h in range(H3):
                    c = 8 + 8 * k + 2 * h
                    for o in range(K):
                        pe.matmul(wa[:, c:c + 2], w3t[:, h, o, fs], A3[:, o, h, :], start=o == 0, stop=o == K - 1)
            for k in range(H3 * K):
                for o in range(K):
                    last = pe.matmul(wa[:, 24 + 2 * k:26 + 2 * k], w4t[:, o, k * P:(k + 1) * P], A4[:, o, :],
                                     start=o == 0, stop=o == K - 1)
            last.then_inc(s_wa, 1)
            pe.wait_ge(s_wa, 2)

            def turn(r, job, col, src):
                return pe.transpose(r.ps(job)[:, col:col + P], src, ident[:, :])

            def xpose(half, h, b):
                r = ring[half]
                if half == "f":
                    src = x_in if h == 0 else xf
                    if h == 0:
                        pe.wait_ge(x_loaded.sem, x_loaded.at(b, 16))
                    else:
                        pe.wait_ge(normed["f"].sem, normed["f"].at(b, T * h))
                elif h == 0:
                    src = xf
                    pe.wait_ge(normed["f"].sem, normed["f"].at(b, 3 * T))
                else:
                    src = ob
                    pe.wait_ge(elu_done.sem, elu_done.at(b, B_HEADS))
                for k in range(K):
                    job = r.job("xpose", h, k)
                    pe.wait_ge(r.drained[job % RING], r.count(b, job) - 1)
                    for t in range(T):
                        last = turn(r, job, t * P, src[:, t, k * P:(k + 1) * P])
                    last.then_inc(r.full[job % RING], 1)
                    yield

            def layer_input(half, h):
                if (half, h) == ("b", 4):
                    return ht, H3 * K
                return (xtf if half == "f" else xtb), K

            def fcols(half, h, b):
                r = ring[half]
                src, tiles = layer_input(half, h)
                wa = wa_of(half, h)
                n = wa.shape[2]
                if (half, h) != ("b", 4):
                    for k in range(K):
                        turned = r.job("xpose", 2 if h == 9 else 0, k)
                        pe.wait_ge(r.drained[turned % RING], r.count(b, turned))
                job = r.job("fcols", h)
                pe.wait_ge(r.drained[job % RING], r.count(b, job) - 1)
                for t in range(T):
                    for k in range(tiles):
                        last = pe.matmul(r.ps(job)[:, t * n:(t + 1) * n], src[:, k, t * P:(t + 1) * P], wa[:, k, :],
                                         start=k == 0, stop=k == tiles - 1)
                last.then_inc(r.full[job % RING], 1)
                yield

            def fbc(half, h, b):
                r = ring[half]
                if half == "f" or h in (0, H3):
                    columns = r.job("fcols", h)
                    pe.wait_ge(r.drained[columns % RING], r.count(b, columns))
                job = r.job("fbc", h)
                pe.wait_ge(r.drained[job % RING], r.count(b, job) - 1)
                for t in range(T):
                    last = turn(r, job, t * P, fcol(half, h, 1)[:, t, :].broadcast_to([P, P]))
                last.then_inc(r.full[job % RING], 1)
                yield

            def wh(half, h, b):
                r = ring[half]
                src, tiles = layer_input(half, h)
                if (half, h) == ("b", 4):
                    pe.wait_ge(elu_done.sem, elu_done.at(b, H3))
                n = O0 if (half, h) == ("f", 0) else D
                per = BANK // n
                for t in range(T):
                    job = r.job("wh", h, t // per)
                    if t % per == 0:
                        pe.wait_ge(r.drained[job % RING], r.count(b, job) - 1)
                    for k in range(tiles):
                        if half == "f":
                            wt = W0[:, k, :] if h == 0 else W2[:, k, :]
                        else:
                            wt = W3[:, k, h, :] if h < H3 else W4[:, k, :]
                        last = pe.matmul(r.ps(job)[:, t % per * n:(t % per + 1) * n], src[:, k, t * P:(t + 1) * P], wt,
                                         start=k == 0, stop=k == tiles - 1)
                    if t % per == per - 1:
                        last.then_inc(r.full[job % RING], 1)
                        yield

            def ptrans(half, h, b):
                r = ring[half]
                for t in range(T):
                    job = r.job("ptrans", h, t)
                    pe.wait_ge(probs[half].sem, probs[half].at(b, T * h + t + 1))
                    pe.wait_ge(r.drained[job % RING], r.count(b, job) - 1)
                    for j in range(T):
                        last = turn(r, job, j * P, zbuf(half, h)[:, t, j * P:(j + 1) * P])
                    last.then_inc(r.full[job % RING], 1)
                    yield

            def attn(half, h, b):
                r = ring[half]
                for t in range(T - RING, T):
                    turned = r.job("ptrans", h, t)
                    pe.wait_ge(r.drained[turned % RING], r.count(b, turned))
                if (half, h) == ("f", 0) or (half, h) == ("f", 9) or (half, h) == ("b", 4):
                    n = O0 if (half, h) == ("f", 0) else D
                    per = BANK // n
                    whs = whf if half == "f" else whb[:, 0]
                    for t in range(T):
                        job = r.job("attn", h, t // per)
                        if t % per == 0:
                            pe.wait_ge(r.drained[job % RING], r.count(b, job) - 1)
                        for j in range(T):
                            last = pe.matmul(r.ps(job)[:, t % per * n:(t % per + 1) * n],
                                             pt(half, h)[:, j, t * P:(t + 1) * P], whs[:, j, 0:n],
                                             start=j == 0, stop=j == T - 1)
                        if t % per == per - 1:
                            last.then_inc(r.full[job % RING], 1)
                            yield
                elif half == "f":
                    m, g = (h - 1) // 4, (h - 1) % 4
                    if h == 1 and later(b):
                        pe.wait_ge(o_ready.sem, o_ready.at(b, 0))
                    for j in range(T):
                        last = pe.matmul(heads_out[m][DH * g:DH * (g + 1), :], whf[:, j, DH * (h - 1):DH * h],
                                         pt(half, h)[:, j, :], start=j == 0, stop=j == T - 1)
                    last.then_inc(heads_done.sem, 1)
                    yield
                else:
                    for k in range(K):
                        job = r.job("attn", h, k)
                        pe.wait_ge(r.drained[job % RING], r.count(b, job) - 1)
                        for j in range(T):
                            last = pe.matmul(r.ps(job)[:, :], whb[:, h % 2, j, k * P:(k + 1) * P],
                                             pt(half, h)[:, j, :], start=j == 0, stop=j == T - 1)
                        last.then_inc(r.full[job % RING], 1)
                        yield

            def zbc(half, h, b):
                r = ring[half]
                if half == "f":
                    pe.wait_ge(recips["f"].sem, recips["f"].at(b, 2))
                    for m in range(K):
                        job = r.job("zbc", 1, m)
                        pe.wait_ge(r.drained[job % RING], r.count(b, job) - 1)
                        for t in range(T):
                            last = turn(r, job, t * P, rz1[:, t, m * P:(m + 1) * P])
                        last.then_inc(r.full[job % RING], 1)
                        yield
                else:
                    pe.wait_ge(recips["b"].sem, recips["b"].at(b, h + 1))
                    job = r.job("zbc", h)
                    pe.wait_ge(r.drained[job % RING], r.count(b, job) - 1)
                    for t in range(T):
                        last = turn(r, job, t * P, RZ["b"][:, h % 2, t:t + 1].broadcast_to([P, P]))
                    last.then_inc(r.full[job % RING], 1)
                    yield

            def scores(h, b):
                m, g = (h - 1) // 4, (h - 1) % 4
                pe.wait_ge(stacked[g].sem, stacked[g].at(b, 64))
                for t in range(T):
                    job = fr.job("scores", h, t)
                    pe.wait_ge(fr.drained[job % RING], fr.count(b, job) - 1)
                    pe.matmul(fr.ps(job)[:, :], stack[0:3 * DH, m, 0, g, t * P:(t + 1) * P],
                                        stack[0:3 * DH, m, 1, g, :], start=True, stop=True).then_inc(fr.full[job % RING], 1)
                    yield

            def project(r, stage, h, b, first, weights, src):
                for m in range(K):
                    job = r.job(stage, h, first + m)
                    pe.wait_ge(r.drained[job % RING], r.count(b, job) - 1)
                    for k in range(K):
                        last = pe.matmul(r.ps(job)[:, :], weights[:, k, m * P:(m + 1) * P], src[:, k, :],
                                         start=k == 0, stop=k == K - 1)
                    last.then_inc(r.full[job % RING], 1)
                    yield

            def project_nodes(r, stage, h, b, weights, src):
                for t in range(T):
                    job = r.job(stage, h, t // 2)
                    if t % 2 == 0:
                        pe.wait_ge(r.drained[job % RING], r.count(b, job) - 1)
                    for k in range(K):
                        last = pe.matmul(r.ps(job)[:, t % 2 * D:(t % 2 + 1) * D], src[:, k, t * P:(t + 1) * P],
                                         weights[:, k, :], start=k == 0, stop=k == K - 1)
                    if t % 2 == 1:
                        last.then_inc(r.full[job % RING], 1)
                        yield

            def steps(half, b):
                for stage, h in STAGES[half] if b is not None else ():
                    if stage == "xpose":
                        yield from xpose(half, h, b)
                    elif stage == "fcols":
                        yield from fcols(half, h, b)
                    elif stage == "fbc":
                        yield from fbc(half, h, b)
                    elif stage == "wh":
                        yield from wh(half, h, b)
                    elif stage == "ptrans":
                        yield from ptrans(half, h, b)
                    elif stage == "attn":
                        yield from attn(half, h, b)
                    elif stage == "zbc":
                        yield from zbc(half, h, b)
                    elif stage == "scores":
                        yield from scores(h, b)
                    elif stage == "qk":
                        for k in range(K):
                            turned = fr.job("xpose", 1, k)
                            pe.wait_ge(fr.drained[turned % RING], fr.count(b, turned))
                        for i, weights in enumerate((WQ, WK)):
                            yield from project(fr, "qk", 1, b, K * i, weights, xtf)
                    elif stage == "v":
                        yield from project_nodes(fr, "v", 1, b, WV, xtf)
                    elif stage == "oproj":
                        pe.wait_ge(o_ready.sem, o_ready.at(b, K))
                        yield from project_nodes(fr, "oproj", 1, b, WO, xtf)
                    elif stage == "w1":
                        for k in range(K):
                            turned = bk.job("xpose", 4, k)
                            pe.wait_ge(bk.drained[turned % RING], bk.count(b, turned))
                        yield from project(bk, "w1", 4, b, 0, FF1, xtb)
                    elif stage == "w2":
                        for k in range(K):
                            hidden = bk.job("w1", 4, k)
                            pe.wait_ge(bk.drained[hidden % RING], bk.count(b, hidden))
                        yield from project_nodes(bk, "w2", 4, b, FF2, ex[:, :].rearrange("p (k n) -> p k n", k=K))

            def program(b_front, b_back):
                take_turns("pe", steps("f", b_front), steps("b", b_back))

            program(0, None)
            program(1, 0)
            with pe.Fori(1, B - 1) as t:
                program(t + 1, t)
            program(None, B - 1)

        @block.scalar
        def _(act):
            act.wait_ge(s_wa, 1)
            act.activation(WA[:, :], heads_out[0][:, 0:40], ACT.Copy).then_inc(s_wa, 1)
            act.wait_ge(s_w, 16 * N_LOADS)

            def copy(dst, src):
                return act.activation(dst, src, ACT.Copy)

            def exp(half, h, b):
                act.wait_ge(logits[half].sem, logits[half].at(b, logit_steps(half, h) + (3 if additive(half, h) else 1)))
                z = zbuf(half, h)
                for t in range(T):
                    total = ZS[half][:, h % 2, t:t + 1] if additive(half, h) else zs1[:, t, h - 1:h]
                    act.activation(z[:, t, :], z[:, t, :], ACT.Exp, bias=NM[half][:, h % 2, t:t + 1],
                                   scale=1.0 if additive(half, h) else SCALE,
                                   accum_out=total).then_inc(probs[half].sem, 1)
                    yield

            def evacuate(r, b, job, dst, src):
                act.wait_ge(r.full[job % RING], r.count(b, job))
                copy(dst, src).then_inc(r.drained[job % RING], 1)
                yield

            def steps(half, b):
                for stage, h in STAGES[half] if b is not None else ():
                    r = ring[half]
                    if stage == "exp":
                        yield from exp(half, h, b)
                    elif stage == "xpose":
                        job = r.job("xpose", h, 0)
                        yield from evacuate(r, b, job, (xtf if half == "f" else xtb)[:, 0, :], r.ps(job)[:, :])
                    elif stage == "fcols":
                        n = wa_of(half, h).shape[2]
                        job = r.job("fcols", h)
                        yield from evacuate(r, b, job, FC[half][:, :, 0:n],
                                 r.ps(job)[:, 0:T * n].rearrange("p (t c) -> p t c", t=T))
                    elif stage == "wh" and (half, h) == ("f", 0):
                        job = r.job("wh", 0)
                        yield from evacuate(r, b, job, whf[:, :, 0:O0], r.ps(job)[:, :].rearrange("p (t n) -> p t n", t=T))
                    elif stage == "wh":
                        job = r.job("wh", h, 0)
                        yield from evacuate(r, b, job, (whf if half == "f" else whb[:, h % 2])[:, 0:2, :],
                                 r.ps(job)[:, :].rearrange("p (t n) -> p t n", t=2))
                    elif stage == "ptrans":
                        for t in range(T):
                            if turned_by_vector(half, h, t):
                                continue
                            if (half, h, t) == ("f", 1, 0):
                                for g in range(4):
                                    act.wait_ge(stacked[g].sem, stacked[g].at(b, 64))
                            job = r.job("ptrans", h, t)
                            yield from evacuate(r, b, job, pt(half, h)[:, :, t * P:(t + 1) * P],
                                     r.ps(job)[:, :].rearrange("p (j i) -> p j i", j=T))
                    elif stage == "qk":
                        for n in range(2 * K):
                            i, m = divmod(n, K)
                            job = r.job("qk", 1, n)
                            act.wait_ge(r.full[job % RING], r.count(b, job))
                            act.activation(parts[:, m, 1 + i, :].bitcast(F32R), r.ps(job)[:, :], ACT.Identity,
                                           bias=BQK[:, i, m:m + 1]).then_inc(high_part.sem, 1)
                            yield
                    elif (half, stage) == ("f", "zbc"):
                        for m in range(K):
                            job = r.job("zbc", 1, m)
                            act.wait_ge(r.full[job % RING], r.count(b, job))
                            copy(rzbf[:, m, :], r.ps(job)[:, :]).then_inc(r.drained[job % RING], 1)
                            yield
                    elif (half, stage) == ("b", "zbc"):
                        job = r.job("zbc", h)
                        act.wait_ge(r.full[job % RING], r.count(b, job))
                        copy(rzbb[:, :], r.ps(job)[:, :]).then_inc(r.drained[job % RING], 1)
                        yield
                    elif (half, stage) == ("b", "attn"):
                        for k in range(K):
                            output = r.job("attn", h, k)
                            act.wait_ge(r.drained[output % RING], r.count(b, output))
                        act.activation(ex[:, :], pre[:, :], ACT.Exp).then_inc(ex_done.sem, 1)
                        yield
                    elif stage == "w1":
                        for m in range(K):
                            job = r.job("w1", 4, m)
                            act.wait_ge(r.full[job % RING], r.count(b, job))
                            act.activation(ex[:, m * N:(m + 1) * N], r.ps(job)[:, :], ACT.Relu,
                                                   bias=B1[:, m:m + 1]).then_inc(r.drained[job % RING], 1)
                            yield

            def program(b_front, b_back):
                take_turns("act", steps("f", b_front), steps("b", b_back))

            program(0, None)
            program(1, 0)
            with act.Fori(1, B - 1) as t:
                program(t + 1, t)
            program(None, B - 1)

        @block.gpsimd
        def _(pool):
            pool.memset(ident[:, :], 0.0).then_inc(s_id, 1)
            pool.wait_ge(s_id, 1)
            pool.affine_select(out=ident[:, :], in_=ident[:, :], compare_op=ALU.not_equal, fill=1.0,
                               base=0, pattern=[[-1, P]], channel_multiplier=1).then_inc(s_id, 1)
            pool.memset(minus_half[:, :], -0.5).then_inc(s_id, 1)
            pool.wait_ge(s_id, 3)
            pool.wait_ge(s_wa, 1)
            pool.wait_ge(s_mask, 1)
            pool.wait_ge(s_w, 16 * N_LOADS)

            def row(v):
                return v[:, :].unsqueeze(1).broadcast_to([P, T, D])

            def steps(half, b):
                for stage, h in STAGES[half] if b is not None else ():
                    r = ring[half]
                    if stage == "bias":
                        if half == "f" or h in (0, H3):
                            columns = r.job("fcols", h)
                            pool.wait_ge(r.drained[columns % RING], r.count(b, columns))
                        back, before = last_user(half, h)
                        if half == "b" and back:
                            if later(b):
                                pool.wait_ge(normed["b"].sem, normed["b"].at(b, 0))
                        elif not back or later(b):
                            turned = r.job("ptrans", before, T - 1)
                            pool.wait_ge(r.full[turned % RING], r.count(b + back, turned))
                        for t in range(T):
                            pool.tensor_tensor(zbuf(half, h)[:, t, :], mask[:, t, :],
                                               fcol(half, h, 0)[:, t, :].broadcast_to([P, N]),
                                               ALU.add).then_inc(biased[half].sem, 1)
                            yield
                    elif stage == "addh":
                        projected = r.job("wh", 0)
                        pool.wait_ge(r.drained[projected % RING], r.count(b, projected))
                        pool.wait_ge(x_loaded.sem, x_loaded.at(b, 16))
                        if later(b):
                            pool.wait_ge(normed["f"].sem, normed["f"].at(b, 0))
                        pool.tensor_tensor(yf[:, :, O0:D], x_in[:, :, O0:D], whf[:, :, 0:O0],
                                           ALU.add).then_inc(added["f"].sem, 1)
                        yield
                    elif stage == "xbo":
                        pool.wait_ge(normed["f"].sem, normed["f"].at(b, T))
                        pool.tensor_tensor(yf[:, :, :], xf[:, :, :], row(BO), ALU.add).then_inc(added["f"].sem, 1)
                        yield
                    elif stage == "xbeta":
                        pool.wait_ge(normed["f"].sem, normed["f"].at(b, 3 * T))
                        if later(b):
                            pool.wait_ge(normed["b"].sem, normed["b"].at(b, 0))
                        pool.tensor_tensor(xb[:, :, :], xf[:, :, :], row(BETA), ALU.add).then_inc(added["b"].sem, 1)
                        yield
                    elif stage == "w2":
                        pool.wait_ge(elu_done.sem, elu_done.at(b, B_HEADS))
                        pool.tensor_tensor(yb[:, :, :], ob[:, :, :], row(B2), ALU.add).then_inc(added["b"].sem, 1)
                        yield
                    elif stage == "affine":
                        pool.wait_ge(normed["b"].sem, normed["b"].at(b, T))
                        pool.tensor_tensor(yb[:, :, :], ob[:, :, :], row(GAMMA), ALU.mult) \
                            .then_inc(added["b"].sem, 1)
                        yield
                    elif stage == "norm":
                        n = h if half == "f" else h - 3
                        pool.wait_ge(stats[half].sem, stats[half].at(b, 3 * n + 3))
                        pool.tensor_tensor(RS[half][:, :], VE[half][:, :], minus_half[:, :],
                                           ALU.pow).then_inc(rstd[half].sem, 1)
                        yield

            def program(b_front, b_back):
                take_turns("pool", steps("f", b_front), steps("b", b_back))

            program(0, None)
            program(1, 0)
            with pool.Fori(1, B - 1) as t:
                program(t + 1, t)
            program(None, B - 1)

        @block.vector
        def _(dve):
            dve.wait_ge(s_adj, 16)
            zb = Z["b"][:, :, :, :].rearrange("p a t n -> p (a t n)")
            dve.tensor_scalar(mask[:, :, :].rearrange("p t n -> p (t n)"), zb[:, 0:T * N].bitcast(I32), FAR, -FAR,
                              ALU.mult, ALU.add).then_inc(s_mask, 1)
            dve.wait_ge(s_mask, 1)
            dve.wait_ge(s_w, 16 * N_LOADS)
            dve.wait_ge(s_wa, 2)

            def evacuate(r, b, job, dst, src):
                dve.wait_ge(r.full[job % RING], r.count(b, job))
                dve.tensor_copy(dst, src).then_inc(r.drained[job % RING], 1)
                yield

            def maxima(half, h, b):
                r = ring[half]
                z, g, ng, nm = zbuf(half, h), G[half][:, h % 2], NG[half][:, h % 2], NM[half][:, h % 2]
                step = logit_steps(half, h)
                if additive(half, h):
                    job = r.job("fbc", h)
                    seen = ahead(dve, r.count(b, job))
                    dve.wait_ge(s_adj, 16)
                    dve.wait_ge(r.full[job % RING], seen)
                    for t in range(T):
                        index = (0 if h == 0 else 1) if half == "f" else h
                        seen = ahead(dve, biased[half].at(b, T * index + t + 1))
                        dve.wait_ge(s_adj, 16)
                        dve.wait_ge(biased[half].sem, seen)
                        last = dve.tensor_tensor_reduce(z[:, t, :], r.ps(job)[:, :], z[:, t, :], 1.0, -3e38,
                                                        ALU.add, ALU.max, g[:, t:t + 1])
                    last.then_inc(r.drained[job % RING], 1)
                    yield
                    dve.wait_ge(r.drained[job % RING], r.count(b, job))
                    dve.tensor_scalar(ng, g, -1.0, None, ALU.mult).then_inc(logits[half].sem, 1)
                    yield
                    flat = z.rearrange("p t n -> p (t n)")
                    dve.scalar_tensor_tensor(out=flat, in0=flat, scalar=slope(half, h), in1=flat,
                                             op0=ALU.mult, op1=ALU.max).then_inc(logits[half].sem, 1)
                    yield
                    dve.wait_ge(logits[half].sem, logits[half].at(b, step + 1))
                    dve.scalar_tensor_tensor(out=nm, in0=ng, scalar=slope(half, h), in1=ng,
                                             op0=ALU.mult, op1=ALU.min).then_inc(logits[half].sem, 1)
                    yield
                else:
                    for t in range(T):
                        job = r.job("scores", h, t)
                        seen = ahead(dve, r.count(b, job))
                        dve.wait_ge(s_adj, 16)
                        dve.wait_ge(r.full[job % RING], seen)
                        dve.tensor_tensor_reduce(z[:, t, :], r.ps(job)[:, :], mask[:, t, :], 1.0, -3e38,
                                                         ALU.add, ALU.max, g[:, t:t + 1]).then_inc(r.drained[job % RING], 1)
                        yield
                    dve.wait_ge(r.drained[job % RING], r.count(b, job))
                    dve.tensor_scalar(nm, g, -SCALE, None, ALU.mult).then_inc(logits[half].sem, 1)
                    yield

            def recip(half, h, b):
                dve.wait_ge(probs[half].sem, probs[half].at(b, T * h + T))
                if (half, h) == ("f", H1):
                    dve.reciprocal(rz1[:, :, :].rearrange("p t (h d) -> p (t h) d", h=H1),
                                   zs1[:, :, :].rearrange("p t h -> p (t h)").unsqueeze(2)
                                   .broadcast_to([P, T * H1, DH])).then_inc(recips["f"].sem, 1)
                    yield
                else:
                    dve.reciprocal(RZ[half][:, h % 2, :], ZS[half][:, h % 2, :]).then_inc(recips[half].sem, 1)
                    yield

            def elu(h, b, dst):
                dve.wait_ge(ex_done.sem, ex_done.at(b, h + 1))
                dve.tensor_scalar(ex[:, :], ex[:, :], 1.0, -1.0, ALU.min, ALU.add).then_inc(elu_low.sem, 1)
                yield
                dve.wait_ge(elu_low.sem, elu_low.at(b, h + 1))
                dve.tensor_tensor(dst, pre[:, :], ex[:, :], ALU.max).then_inc(elu_done.sem, 1)
                yield

            def attn(half, h, b):
                r = ring[half]
                if half == "f" and not additive(half, h):
                    return
                rz = RZ[half][:, h % 2]
                if half == "f":
                    dve.wait_ge(recips["f"].sem, recips["f"].at(b, 1 if h == 0 else 3))
                    n = O0 if h == 0 else D
                    per = BANK // n
                    src = x_in if h == 0 else xf
                    for t in range(T):
                        job = r.job("attn", h, t // per)
                        if t % per == 0:
                            dve.wait_ge(r.full[job % RING], r.count(b, job))
                        last = dve.scalar_tensor_tensor(out=yf[:, t, 0:n], in0=r.ps(job)[:, t % per * n:(t % per + 1) * n],
                                                        scalar=rz[:, t:t + 1], in1=src[:, t, 0:n],
                                                        op0=ALU.mult, op1=ALU.add)
                        if t % per == per - 1:
                            last.then_inc(r.drained[job % RING], 1)
                            yield
                elif h < H3:
                    spread = r.job("zbc", h)
                    dve.wait_ge(r.drained[spread % RING], r.count(b, spread))
                    for k in range(K):
                        job = r.job("attn", h, k)
                        dve.wait_ge(r.full[job % RING], r.count(b, job))
                        dve.tensor_tensor(pre[:, k * N:(k + 1) * N], r.ps(job)[:, :], rzbb[:, :], ALU.mult).then_inc(r.drained[job % RING], 1)
                        yield
                    yield from elu(h, b, ht[:, K * h:K * (h + 1), :].rearrange("p k n -> p (k n)"))
                else:
                    dve.wait_ge(recips["b"].sem, recips["b"].at(b, B_HEADS))
                    for t in range(T):
                        job = r.job("attn", h, t // 2)
                        if t % 2 == 0:
                            dve.wait_ge(r.full[job % RING], r.count(b, job))
                        last = dve.tensor_scalar(pre[:, t * D:(t + 1) * D], r.ps(job)[:, t % 2 * D:(t % 2 + 1) * D],
                                                 rz[:, t:t + 1], None, ALU.mult)
                        if t % 2 == 1:
                            last.then_inc(r.drained[job % RING], 1)
                            yield
                    if later(b):
                        dve.wait_ge(stored.sem, stored.at(b, 0))
                    yield from elu(h, b, ob[:, :, :].rearrange("p t d -> p (t d)"))

            def norm(half, n, y, dst, b):
                for t in range(T):
                    last = dve.bn_stats(ST[half][:, t, :], y[:, t, :])
                last.then_inc(stats[half].sem, 1)
                yield
                seen = ahead(dve, stats[half].at(b, 3 * n + 1))
                dve.wait_ge(s_adj, 16)
                dve.wait_ge(stats[half].sem, seen)
                for t in range(T):
                    last = dve.bn_aggr(MV[half][:, t, :], ST[half][:, t, :])
                last.then_inc(stats[half].sem, 1)
                yield
                dve.wait_ge(stats[half].sem, stats[half].at(b, 3 * n + 2))
                dve.tensor_scalar(VE[half][:, :], MV[half][:, :, 1], EPS, None, ALU.add).then_inc(stats[half].sem, 1)
                yield
                dve.wait_ge(rstd[half].sem, rstd[half].at(b, n + 1))
                for t in range(T):
                    dve.tensor_scalar(dst[:, t, :], y[:, t, :], MV[half][:, t, 0:1], RS[half][:, t:t + 1],
                                      ALU.subtract, ALU.mult).then_inc(normed[half].sem, 1)
                    yield

            def steps(half, b):
                for stage, h in STAGES[half] if b is not None else ():
                    r = ring[half]
                    if stage == "fbc" or stage == "scores":
                        yield from maxima(half, h, b)
                    elif stage == "xpose":
                        job = r.job("xpose", h, 1)
                        yield from evacuate(r, b, job, (xtf if half == "f" else xtb)[:, 1, :], r.ps(job)[:, :])
                    elif stage == "wh" and (half, h) != ("f", 0):
                        job = r.job("wh", h, 1)
                        yield from evacuate(r, b, job, (whf if half == "f" else whb[:, h % 2])[:, 2:4, :],
                                 r.ps(job)[:, :].rearrange("p (t n) -> p t n", t=2))
                    elif stage == "ptrans":
                        for t in range(T):
                            if not turned_by_vector(half, h, t):
                                continue
                            if (half, h, t) == ("f", 1, 1):
                                for g in range(4):
                                    dve.wait_ge(stacked[g].sem, stacked[g].at(b, 64))
                            job = r.job("ptrans", h, t)
                            yield from evacuate(r, b, job, pt(half, h)[:, :, t * P:(t + 1) * P],
                                     r.ps(job)[:, :].rearrange("p (j i) -> p j i", j=T))
                        if additive(half, h) or h == H1:
                            yield from recip(half, h, b)
                    elif stage == "attn":
                        yield from attn(half, h, b)
                    elif stage == "qk":
                        for n in range(2 * K):
                            i, m = divmod(n, K)
                            job = r.job("qk", 1, n)
                            dve.wait_ge(high_part.sem, high_part.at(b, n + 1))
                            dve.scalar_tensor_tensor(
                                out=parts[:, m, 3 * i, :].bitcast(F32R), in0=r.ps(job)[:, :],
                                scalar=BQK[:, i, m:m + 1], in1=parts[:, m, 1 + i, :],
                                op0=ALU.add, op1=ALU.subtract).then_inc(r.drained[job % RING], 1)
                            yield
                    elif stage == "v":
                        for n in range(2):
                            job = r.job("v", 1, n)
                            dve.wait_ge(r.full[job % RING], r.count(b, job))
                            dve.tensor_tensor(whf[:, 2 * n:2 * n + 2, :],
                                                      r.ps(job)[:, :].rearrange("p (t n) -> p t n", t=2),
                                                      BV[:, :].unsqueeze(1).broadcast_to([P, 2, D]), ALU.add).then_inc(r.drained[job % RING], 1)
                            yield
                    elif (half, stage) == ("f", "zbc"):
                        dve.wait_ge(heads_done.sem, heads_done.at(b, H1))
                        for m in range(K):
                            spread = r.job("zbc", 1, m)
                            dve.wait_ge(r.drained[spread % RING], r.count(b, spread))
                        for m in range(K):
                            dve.tensor_tensor(xtf[:, m, :], heads_out[m][:, :], rzbf[:, m, :],
                                              ALU.mult).then_inc(o_ready.sem, 1)
                            yield
                    elif stage == "oproj" or stage == "w2":
                        y = yf if stage == "oproj" else yb
                        dve.wait_ge(added[half].sem, added[half].at(b, 2))
                        for n in range(2):
                            job = r.job(stage, h, n)
                            dve.wait_ge(r.full[job % RING], r.count(b, job))
                            dve.tensor_tensor(y[:, 2 * n:2 * n + 2, :],
                                                      r.ps(job)[:, :].rearrange("p (t n) -> p t n", t=2),
                                                      y[:, 2 * n:2 * n + 2, :], ALU.add).then_inc(r.drained[job % RING], 1)
                            yield
                    elif (half, stage) == ("f", "norm"):
                        for job in {0: [r.job("attn", 0)], 1: [r.job("oproj", 1, k) for k in range(2)],
                                    2: [r.job("attn", 9, k) for k in range(2)]}[h]:
                            dve.wait_ge(r.drained[job % RING], r.count(b, job))
                        if h == 0:
                            dve.wait_ge(added["f"].sem, added["f"].at(b, 1))
                            if later(b):
                                dve.wait_ge(added["b"].sem, added["b"].at(b - 1, 1))
                                turned = bk.job("xpose", 0, K - 1)
                                dve.wait_ge(bk.full[turned % RING], bk.count(b - 1, turned))
                        yield from norm("f", h, yf, xf, b)
                    elif (half, stage, h) == ("b", "norm", 3):
                        for k in range(2):
                            job = r.job("w2", 4, k)
                            dve.wait_ge(r.drained[job % RING], r.count(b, job))
                        yield from norm("b", 0, yb, ob, b)
                    elif (half, stage, h) == ("b", "norm", 4):
                        dve.wait_ge(summed.sem, summed.at(b, 1))
                        yield from norm("b", 1, yb, ob, b)
                    elif stage == "affine":
                        dve.wait_ge(added["b"].sem, added["b"].at(b, 3))
                        dve.tensor_tensor(yb[:, :, :], yb[:, :, :], xb[:, :, :], ALU.add).then_inc(summed.sem, 1)
                        yield

            def program(b_front, b_back):
                take_turns("dve", steps("f", b_front), steps("b", b_back))

            program(0, None)
            program(1, 0)
            with dve.Fori(1, B - 1) as t:
                program(t + 1, t)
            program(None, B - 1)


N_LOADS = 25


def kernel(**inputs):
    import numpy as np
    import concourse.bacc as bacc
    from concourse.bass_utils import run_bass_kernel_spmd as run

    a = {k: np.asarray(v) for k, v in inputs.items()}

    def tiles(m):
        return m.reshape(m.shape[0] // P, P, *m.shape[1:]).swapaxes(0, 1)

    def rows(v):
        return np.broadcast_to(v, (P, v.shape[0]))

    h0, w3, a3 = a["L0_gnn_a"], a["L3_gnn_W_heads"], a["L3_gnn_a_heads"]
    data = {
        "x": a["x"].reshape(B, T, P, D).swapaxes(1, 2), "adj": tiles(a["adj"]).reshape(P, T * N),
        "w0": tiles(a["L0_gnn_W"]), "w0t": a["L0_gnn_W"].T, "a0": h0[:, :, 0].T,
        "wq": tiles(a["L1_gnn_Wq"].T), "wk": tiles(a["L1_gnn_Wk"].T), "wv": tiles(a["L1_gnn_Wv"].T),
        "wo": tiles(a["L1_gnn_Wo"].T),
        "bqk": np.stack([tiles(a["L1_gnn_bq"]), tiles(a["L1_gnn_bk"])], 1),
        "bv": rows(a["L1_gnn_bv"]), "bo": rows(a["L1_gnn_bo"]),
        "w2": tiles(a["L2_gnn_W"]), "w2t": tiles(a["L2_gnn_W"].T).reshape(P, K * D),
        "a2": tiles(np.stack([a["L2_gnn_a_src"], a["L2_gnn_a_dst"]], 1)),
        "w3": tiles(w3.transpose(1, 0, 2)),
        "w3t": w3.transpose(0, 2, 1).reshape(H3, K, P, D).transpose(2, 0, 1, 3).reshape(P, H3 * K * D),
        "a3": tiles(a3.reshape(H3, 2, D).transpose(2, 0, 1)),
        "w4": tiles(a["L3_gnn_W_out"]), "w4t": tiles(a["L3_gnn_W_out"].T).reshape(P, K * H3 * D),
        "a4": tiles(a["L3_gnn_a_out"].reshape(2, D).T),
        "f1": tiles(a["L3_gnn_w1"]), "b1": tiles(a["L3_gnn_b1"]), "f2": tiles(a["L3_gnn_w2"]),
        "b2": rows(a["L3_gnn_b2"]), "gamma": rows(a["L3_gnn_ln_gamma"]), "beta": rows(a["L3_gnn_ln_beta"]),
    }
    data = {k: np.ascontiguousarray(v) for k, v in data.items()}
    nc = bacc.Bacc("TRN2", target_bir_lowering=False, num_devices=1)
    dram = {k: nc.dram_tensor(k + "_dram", v.shape, mybir.dt.from_np(v.dtype), kind="ExternalInput").ap()
            for k, v in data.items()}
    out = nc.dram_tensor("out_dram", (B, P, T, D), F32, kind="ExternalOutput").ap()
    graph_layers(nc, dram.pop("x"), dram.pop("adj"), dram, out)
    r = run(nc, [{k + "_dram": v for k, v in data.items()}], core_ids=[0])
    got = r.results[0]["out_dram"]
    return np.ascontiguousarray(got.swapaxes(1, 2)).reshape(B, N, D)
```

```python
from contextlib import ExitStack

import concourse.bass as bass
from concourse import mybir

F32 = mybir.dt.float32
F32R = mybir.dt.float32r
BF16 = mybir.dt.bfloat16
I32 = mybir.dt.int32
ALU = mybir.AluOpType
ACT = mybir.ActivationFunctionType

P = 128
B, N, D = 16, 512, 256
T = N // P
K = D // P
O0 = D // 2
H1 = 8
DH = D // H1
H3 = 4
BANK = 512
RING = 3
FAR = float(2 ** 60)
EPS = 1e-5
SCALE = float(DH) ** -0.5
SLOPE = {"L0": 0.2, "L2": 0.2, "L3": 0.01}

F_HEADS, B_HEADS = H1 + 2, H3 + 1


def front_stages():
    s = [("xpose", 0), ("wh", 0), ("bias", 0), ("fbc", 0), ("addh", 0), ("exp", 0),
         ("ptrans", 0), ("attn", 0), ("norm", 0),
         ("xbo", 1), ("xpose", 1), ("qk", 1), ("v", 1), ("scores", 1), ("scores", 2)]
    for h in range(1, H1 + 1):
        s += [("exp", h), ("ptrans", h)]
        s += [("scores", h + 2)] if h + 2 <= H1 else []
        s += [("attn", h)] if h % 2 == 0 else []
    s += [("zbc", 1), ("oproj", 1), ("norm", 1),
          ("xpose", 2), ("wh", 9), ("bias", 9), ("fbc", 9), ("exp", 9),
          ("ptrans", 9), ("attn", 9), ("norm", 2)]
    return s


def back_stages():
    s = [("xbeta", 0), ("xpose", 0), ("wh", 0), ("bias", 0), ("fbc", 0), ("wh", 1), ("exp", 0)]
    for h in range(H3):
        s += [("ptrans", h), ("zbc", h)]
        s += [("bias", h + 1), ("fbc", h + 1), ("exp", h + 1)] if h + 1 < H3 else []
        s += [("attn", h)]
        s += [("wh", h + 2)] if h + 2 < H3 else []
    s += [("wh", 4), ("bias", 4), ("fbc", 4), ("exp", 4), ("ptrans", 4), ("attn", 4),
          ("xpose", 4), ("w1", 4), ("w2", 4), ("norm", 3), ("norm", 4), ("store", 4)]
    return s


def banks(half, stage, h):
    if stage in ("scores", "ptrans"):
        return T
    if stage == "fbc":
        return 1
    if stage == "wh":
        return 2 if (half, h) == ("f", 0) else T
    if stage == "attn":
        return (1 if h == 0 else 2 if h == 9 else 0) if half == "f" else 2
    if stage == "zbc":
        return 2 if half == "f" else 1
    return {"xpose": 2, "qk": 4, "v": 2, "oproj": 2, "w1": 2, "w2": 2}.get(stage, 0)


STAGES = {"f": front_stages(), "b": back_stages()}

TURNS = {
    "sp": (
        2, 1),
    "pe": (
        2, 1, 1, 1, 2, 7, 4, 1, 1, 9, 2, 1, 3, 3, 2, 4, 1, 1, 2, 1, 1, 2, 1, 3, 4, 1, 4, 1, 2, 1, 1, 2, 1,
        1, 1, 1, 1, 1, 2, 1, 2, 2, 7, 1, 2, 1, 2, 2, 6, 1, 7, 1, 1, 1, 3, 1, 5, 1, 8, 1, 7, 2, 1, 2, 1, 2,
        5, 1, 1, 1, 1, 3, 2, 1, 4),
    "act": (
        2, 3, 5, 1, 2, 10, 1, 1, 1, 3, 2, 1, 1, 10, 2, 1, 3, 1, 2, 1, 1, 2, 2, 1, 1, 1, 1, 3, 1, 3, 7, 1, 2,
        1, 6, 1, 3, 1, 9, 1, 10, 1, 1, 6, 1, 1, 2, 3, 7),
    "pool": (
        0, 1, 5, 6, 1, 7, 1, 7, 3, 1, 2, 2, 1),
    "dve": (
        1, 1, 6, 1, 1, 1, 4, 5, 2, 6, 1, 2, 1, 1, 1, 1, 1, 2, 1, 1, 2, 3, 2, 6, 2, 2, 2, 2, 2, 10, 1, 2, 1,
        1, 2, 1, 1, 1, 5, 1, 1, 1, 1, 1, 2, 1, 3, 6, 1, 1, 1, 5, 2, 1, 3, 2, 3, 1, 5, 1, 3, 1, 2, 1, 1, 1,
        9, 1, 4, 1, 3, 3, 2, 1, 1, 5, 2, 1, 1, 2, 5, 1, 3, 1, 1, 2, 2, 1, 9, 1, 1, 1, 2, 7, 1, 2, 1, 2, 3,
        4, 4),
}


def take_turns(engine, front, back):
    for n, count in enumerate(TURNS[engine]):
        for _ in range(count):
            next((front, back)[n % 2], None)
    for half in (front, back):
        assert next(half, half) is half


def first_jobs(half, stages):
    at, first = 0, {}
    for s, h in stages:
        if banks(half, s, h):
            first[s, h] = at
            at += banks(half, s, h)
    return first, at


class Count:

    def __init__(self, sem, per_graph):
        self.sem, self.per_graph = sem, per_graph

    def at(self, b, n):
        return b * self.per_graph + n


class Ring:

    def __init__(self, ctx, nc, half, stages):
        self.first, self.jobs = first_jobs(half, stages)
        self.bank = [ctx.enter_context(nc.psum_tensor(f"{half}_ring{k}", [P, BANK], F32)) for k in range(RING)]
        self.uses = [(self.jobs - k + RING - 1) // RING for k in range(RING)]
        self.full = [ctx.enter_context(nc.semaphore(f"{half}_full{k}")) for k in range(RING)]
        self.drained = [ctx.enter_context(nc.semaphore(f"{half}_drained{k}")) for k in range(RING)]

    def job(self, stage, h, n=0):
        return self.first[stage, h] + n

    def ps(self, job):
        return self.bank[job % RING]

    def count(self, b, job):
        return b * self.uses[job % RING] + job // RING + 1


def graph_layers(nc, x, adj, w, out):
    ctx = ExitStack()
    with ctx:
        def sb(name, shape, dt=F32):
            return ctx.enter_context(nc.sbuf_tensor(name, shape, dt))

        def sem(name):
            return ctx.enter_context(nc.semaphore(name))

        fr = Ring(ctx, nc, "f", STAGES["f"])
        bk = Ring(ctx, nc, "b", STAGES["b"])
        ring = {"f": fr, "b": bk}
        heads_out = [ctx.enter_context(nc.psum_tensor(f"heads_out{k}", [P, BANK], F32)) for k in range(K)]

        W0 = sb("W0", [P, K, O0 + 2])
        WQ, WK, WV, WO = (sb(n, [P, K, D]) for n in ("WQ", "WK", "WV", "WO"))
        W2 = sb("W2", [P, K, D + 2])
        W3 = sb("W3", [P, K, H3, D + 2])
        W4 = sb("W4", [P, H3 * K, D + 2])
        FF1, FF2 = sb("FF1", [P, K, D]), sb("FF2", [P, K, D])
        A0, A2, A3, A4 = sb("A0", [P, 2]), sb("A2", [P, K, 2]), sb("A3", [P, K, H3, 2]), sb("A4", [P, K, 2])
        BQK, B1 = sb("BQK", [P, 2, K]), sb("B1", [P, K])
        BV, BO, B2, GAMMA, BETA = (sb(n, [P, D]) for n in ("BV", "BO", "B2", "GAMMA", "BETA"))
        mask = sb("mask", [P, T, N], BF16)
        ident = sb("ident", [P, P])
        minus_half = sb("minus_half", [P, T])

        x_in = sb("x_in", [P, T, D])
        xf, yf = sb("xf", [P, T, D]), sb("yf", [P, T, D])
        xtf = sb("xtf", [P, K, N])
        whf = sb("whf", [P, T, D + 2])
        ptf = sb("ptf", [P, 2, T, N])
        parts = ptf
        stack = sb("stack", [P, K, 2, H1 // K, N], F32R)
        rzbf = sb("rzbf", [P, K, N])
        xb, yb, ob = sb("xb", [P, T, D]), sb("yb", [P, T, D]), sb("ob", [P, T, D])
        xtb = sb("xtb", [P, K, N])
        whb = sb("whb", [P, 2, T, D + 2])
        ptb = sb("ptb", [P, T, N])
        rzbb = sb("rzbb", [P, N])
        ht = sb("ht", [P, H3 * K, N])
        pre, ex = sb("pre", [P, K * N]), sb("ex", [P, K * N])
        Z = {h: sb(f"Z{h}", [P, 2, T, N]) for h in "fb"}
        G = {h: sb(f"G{h}", [P, 2, T]) for h in "fb"}
        NG = {h: sb(f"NG{h}", [P, 2, T]) for h in "fb"}
        NM = {h: sb(f"NM{h}", [P, 2, T]) for h in "fb"}
        ZS = {h: sb(f"ZS{h}", [P, 2, T]) for h in "fb"}
        RZ = {h: sb(f"RZ{h}", [P, 2, T]) for h in "fb"}
        zs1, rzs = sb("zs1", [P, T, H1]), sb("rzs", [P, T, H1])
        rz1 = xtf[:, :, :].rearrange("p k (a d) -> p (k a) d", a=K)
        ST = {h: sb(f"ST{h}", [P, T, 6]) for h in "fb"}
        MV = {h: sb(f"MV{h}", [P, T, 2]) for h in "fb"}
        VE = {h: sb(f"VE{h}", [P, T]) for h in "fb"}
        RS = {h: sb(f"RS{h}", [P, T]) for h in "fb"}

        s_early = sem("first_weights_loaded")
        s_w = sem("weights_loaded")
        s_adj = sem("adjacency_loaded")
        s_id = sem("constants_made")
        s_wa = sem("attention_weights")
        s_mask = sem("mask_made")
        x_loaded = Count(sem("x_loaded"), 16)
        stacked = [Count(sem(f"stacked{r}"), 4 * 16) for r in range(4)]
        stored = Count(sem("stored"), 16)
        biased = {"f": Count(sem("f_biased"), 2 * T), "b": Count(sem("b_biased"), B_HEADS * T)}
        logits = {"f": Count(sem("f_logits"), 2 * (2 + T) + H1), "b": Count(sem("b_logits"), (2 + T) * B_HEADS)}
        probs = {"f": Count(sem("f_probs"), F_HEADS * T), "b": Count(sem("b_probs"), B_HEADS * T)}
        recips = {"f": Count(sem("f_recips"), 3), "b": Count(sem("b_recips"), B_HEADS)}
        stats = {"f": Count(sem("f_stats"), 3 * 3), "b": Count(sem("b_stats"), 4 + 3)}
        rstd = {"f": Count(sem("f_rstd"), 3), "b": Count(sem("b_rstd"), 2)}
        normed = {"f": Count(sem("f_normed"), 3 * T), "b": Count(sem("b_normed"), 2 * T)}
        added = {"f": Count(sem("f_added"), 2), "b": Count(sem("b_added"), 2)}
        high_part = Count(sem("high_part"), 4)
        spread = Count(sem("spread"), 1)
        heads_done = Count(sem("heads_done"), H1)
        o_ready = Count(sem("o_ready"), K)
        ex_done = Count(sem("ex_done"), B_HEADS)
        elu_low = Count(sem("elu_low"), B_HEADS)
        elu_done = Count(sem("elu_done"), B_HEADS)

        def stat_steps(half, n):
            return (4 if half == "b" else 3) * n

        def logit_steps(half, h):
            if half == "b":
                return (2 + T) * h
            return 0 if h == 0 else 2 + T + (h - 1)

        def zbuf(half, h):
            return Z[half][:, h % 2]

        def pt(half, h):
            return ptf[:, h % 2] if half == "f" else ptb[:, :, :]

        def last_user(half, h):
            return (0, h - 2) if h >= 2 else (-1, F_HEADS - 2 + h)

        def additive(half, h):
            return half == "b" or h in (0, 9)

        def turned_by_vector(half, h, t):
            return t == 3 if additive(half, h) else t % 2 == 1

        def slope(half, h):
            return SLOPE["L3"] if half == "b" else SLOPE["L0"]

        def projected(half, h):
            if (half, h) == ("f", 0):
                return whf[:, :, 0:O0 + 2], O0
            return (whf[:, :, :] if half == "f" else whb[:, h % 2]), D

        def ahead(eng, value):
            if not isinstance(value, int):
                eng.lower_val(value)
            return value

        def later(b):
            return not (isinstance(b, int) and b == 0)

        block = ctx.enter_context(nc.Block())

        @block.sync
        def _(sp):
            zf = Z["f"][:, :, :, :].rearrange("p a t n -> p (a t n)")
            zb = Z["b"][:, :, :, :].rearrange("p a t n -> p (a t n)")
            sp.dma_start(x_in[:, :, :], x[0]).then_inc(x_loaded.sem, 16)
            sp.dma_start(zb[:, 0:T * N].bitcast(I32), adj).then_inc(s_adj, 16)
            loads = [(A0, "a0"), (A2, "a2"), (A3, "a3"), (A4, "a4"), (zf[:, 0:256], "w0t"), (zf[:, 256:768], "w2t"),
                     (zf[:, T * N:2 * T * N], "w3t"), (zb[:, T * N:2 * T * N], "w4t"),
                     (W0, "w0"), (BQK, "bqk"), (WQ, "wq"), (WK, "wk"), (WV, "wv"), (BV, "bv"), (WO, "wo"), (BO, "bo"),
                     (W2, "w2"), (W3, "w3"), (W4, "w4"), (FF1, "f1"), (B1, "b1"), (FF2, "f2"), (B2, "b2"),
                     (GAMMA, "gamma"), (BETA, "beta")]
            assert len(loads) == N_LOADS
            for dst, name in loads:
                dst = dst[(slice(None),) * len(dst.shape)]
                if name in ("w0", "w2", "w3", "w4"):
                    dst = dst[..., 0:dst.shape[-1] - 2]
                early = name[0] == "a" or name.endswith("t") or name == "w0"
                sp.dma_start(dst, w[name]).then_inc(s_early if early else s_w, 16)

            def one(a, b):
                return a[bass.ds(b, 1)].rearrange("o p t d -> (o p) t d")

            def steps(half, b):
                for stage, h in STAGES[half] if b is not None else ():
                    if (half, stage) == ("f", "v"):
                        sent = fr.job("qk", 1, 3)
                        seen = ahead(sp, fr.count(b, sent))
                        sp.wait_ge(s_adj, 16)
                        sp.wait_ge(fr.drained[sent % RING], seen)
                        for r in range(4):
                            rows = slice(DH * r, DH * (r + 1))
                            done = stacked[r].sem
                            for q in range(2):
                                sp.dma_start(stack[0:DH, :, q, r, :].bitcast(F32),
                                             parts[rows, :, 1 + q]).then_inc(done, 16)
                            for g, first in ((1, 1), (2, 0)):
                                src = parts[rows].rearrange("p m (a c) n -> p c (m a) n", c=2)
                                sp.dma_start(stack[DH * g:DH * (g + 1), :, :, r, :]
                                             .rearrange("p m q n -> p (m q) n").bitcast(F32),
                                             src[:, first]).then_inc(done, 16)
                        yield
                    if (half, stage, h) == ("f", "norm", 0) and not (isinstance(b, int) and b == B - 1):
                        seen = ahead(sp, normed["f"].at(b, T))
                        sp.wait_ge(s_adj, 16)
                        sp.wait_ge(normed["f"].sem, seen)
                        src = x[b + 1] if isinstance(b, int) else one(x, b + 1)
                        sp.dma_start(x_in[:, :, :], src).then_inc(x_loaded.sem, 16)
                        yield
                    if (half, stage) == ("b", "store"):
                        seen = ahead(sp, normed["b"].at(b, 2 * T))
                        sp.wait_ge(s_adj, 16)
                        sp.wait_ge(normed["b"].sem, seen)
                        dst = out[b] if isinstance(b, int) else one(out, b)
                        sp.dma_start(dst, ob[:, :, :]).then_inc(stored.sem, 16)
                        yield

            def program(b_front, b_back):
                take_turns("sp", steps("f", b_front), steps("b", b_back))

            program(0, None)
            program(1, 0)
            with sp.Fori(1, B - 2) as t:
                program(t + 1, t)
            program(B - 1, B - 2)
            program(None, B - 1)
            sp.wait_ge(stored.sem, stored.at(B - 1, 16))

        @block.tensor
        def _(pe):
            pe.wait_ge(s_early, 16 * N_EARLY)
            pe.wait_ge(s_id, 3)
            zf = Z["f"][:, :, :, :].rearrange("p a t n -> p (a t n)")
            zb = Z["b"][:, :, :, :].rearrange("p a t n -> p (a t n)")
            w0t, w2t = zf[:, 0:256], zf[:, 256:768].rearrange("p (o f) -> p o f", o=K)
            w3t = zf[:, T * N:2 * T * N].rearrange("p (h o f) -> p h o f", h=H3, o=K)
            w4t = zb[:, T * N:2 * T * N].rearrange("p (o f) -> p o f", o=K)
            wa = heads_out[0]
            for k in range(K):
                fs = slice(k * P, (k + 1) * P)
                pe.matmul(wa[:, 2 * k:2 * k + 2], w0t[:, fs], A0[:, :], start=True, stop=True)
                for o in range(K):
                    pe.matmul(wa[:, 4 + 2 * k:6 + 2 * k], w2t[:, o, fs], A2[:, o, :], start=o == 0, stop=o == K - 1)
                for h in range(H3):
                    c = 8 + 8 * k + 2 * h
                    for o in range(K):
                        pe.matmul(wa[:, c:c + 2], w3t[:, h, o, fs], A3[:, o, h, :], start=o == 0, stop=o == K - 1)
            for k in range(H3 * K):
                for o in range(K):
                    last = pe.matmul(wa[:, 24 + 2 * k:26 + 2 * k], w4t[:, o, k * P:(k + 1) * P], A4[:, o, :],
                                     start=o == 0, stop=o == K - 1)
            last.then_inc(s_wa, 1)
            pe.wait_ge(s_wa, 5)

            def turn(r, job, col, src):
                return pe.transpose(r.ps(job)[:, col:col + P], src, ident[:, :])

            def xpose(half, h, b):
                r = ring[half]
                if half == "f":
                    src = x_in if h == 0 else xf
                    if h == 0:
                        pe.wait_ge(x_loaded.sem, x_loaded.at(b, 16))
                    else:
                        pe.wait_ge(normed["f"].sem, normed["f"].at(b, T * h))
                elif h == 0:
                    src = xf
                    pe.wait_ge(normed["f"].sem, normed["f"].at(b, 3 * T))
                else:
                    src = ob
                    pe.wait_ge(elu_done.sem, elu_done.at(b, B_HEADS))
                for k in range(K):
                    job = r.job("xpose", h, k)
                    pe.wait_ge(r.drained[job % RING], r.count(b, job) - 1)
                    for t in range(T):
                        last = turn(r, job, t * P, src[:, t, k * P:(k + 1) * P])
                    last.then_inc(r.full[job % RING], 1)
                    yield

            def layer_input(half, h):
                if (half, h) == ("b", 4):
                    return ht, H3 * K
                return (xtf if half == "f" else xtb), K

            def fbc(half, h, b):
                r = ring[half]
                whs, n = projected(half, h)
                job = r.job("fbc", h)
                pe.wait_ge(r.drained[job % RING], r.count(b, job) - 1)
                for t in range(T):
                    node = r.job("wh", h, t * banks(half, "wh", h) // T)
                    pe.wait_ge(r.drained[node % RING], r.count(b, node))
                    last = turn(r, job, t * P, whs[:, t, n + 1:n + 2].broadcast_to([P, P]))
                last.then_inc(r.full[job % RING], 1)
                yield

            def wh(half, h, b):
                r = ring[half]
                src, tiles = layer_input(half, h)
                if (half, h) == ("b", 4):
                    pe.wait_ge(elu_done.sem, elu_done.at(b, H3))
                elif half == "f" or h == 0:
                    for k in range(K):
                        turned = r.job("xpose", 2 if h == 9 else 0, k)
                        pe.wait_ge(r.drained[turned % RING], r.count(b, turned))
                n = projected(half, h)[1] + 2
                per = T // banks(half, "wh", h)
                for t in range(T):
                    job = r.job("wh", h, t // per)
                    if t % per == 0:
                        pe.wait_ge(r.drained[job % RING], r.count(b, job) - 1)
                    for k in range(tiles):
                        if half == "f":
                            wt = W0[:, k, :] if h == 0 else W2[:, k, :]
                        else:
                            wt = W3[:, k, h, :] if h < H3 else W4[:, k, :]
                        last = pe.matmul(r.ps(job)[:, t % per * n:(t % per + 1) * n], src[:, k, t * P:(t + 1) * P], wt,
                                         start=k == 0, stop=k == tiles - 1)
                    if t % per == per - 1:
                        last.then_inc(r.full[job % RING], 1)
                        yield

            def ptrans(half, h, b):
                r = ring[half]
                for t in range(T):
                    job = r.job("ptrans", h, t)
                    pe.wait_ge(probs[half].sem, probs[half].at(b, T * h + t + 1))
                    pe.wait_ge(r.drained[job % RING], r.count(b, job) - 1)
                    for j in range(T):
                        last = turn(r, job, j * P, zbuf(half, h)[:, t, j * P:(j + 1) * P])
                    last.then_inc(r.full[job % RING], 1)
                    yield

            def attn(half, h, b):
                r = ring[half]
                for t in range(T - RING, T):
                    turned = r.job("ptrans", h, t)
                    pe.wait_ge(r.drained[turned % RING], r.count(b, turned))
                if (half, h) == ("f", 0) or (half, h) == ("f", 9) or (half, h) == ("b", 4):
                    n = O0 if (half, h) == ("f", 0) else D
                    per = BANK // n
                    whs = projected(half, h)[0]
                    for t in range(T):
                        job = r.job("attn", h, t // per)
                        if t % per == 0:
                            pe.wait_ge(r.drained[job % RING], r.count(b, job) - 1)
                        for j in range(T):
                            last = pe.matmul(r.ps(job)[:, t % per * n:(t % per + 1) * n],
                                             pt(half, h)[:, j, t * P:(t + 1) * P], whs[:, j, 0:n],
                                             start=j == 0, stop=j == T - 1)
                        if t % per == per - 1:
                            last.then_inc(r.full[job % RING], 1)
                            yield
                elif half == "f":
                    m = (h - 1) // 4
                    if h == 2 and later(b):
                        pe.wait_ge(o_ready.sem, o_ready.at(b, 0))
                    for j in range(T):
                        for head in (h - 1, h):
                            g = (head - 1) % 4
                            last = pe.matmul(heads_out[m][DH * g:DH * (g + 1), :],
                                             whf[:, j, DH * (head - 1):DH * head],
                                             pt(half, head)[:, j, :], start=j == 0, stop=j == T - 1)
                            if j == T - 1:
                                last.then_inc(heads_done.sem, 1)
                    yield
                else:
                    for k in range(K):
                        job = r.job("attn", h, k)
                        pe.wait_ge(r.drained[job % RING], r.count(b, job) - 1)
                        for j in range(T):
                            last = pe.matmul(r.ps(job)[:, :], whb[:, h % 2, j, k * P:(k + 1) * P],
                                             pt(half, h)[:, j, :], start=j == 0, stop=j == T - 1)
                        last.then_inc(r.full[job % RING], 1)
                        yield

            def zbc(half, h, b):
                r = ring[half]
                if half == "f":
                    pe.wait_ge(spread.sem, spread.at(b, 1))
                    for m in range(K):
                        job = r.job("zbc", 1, m)
                        pe.wait_ge(r.drained[job % RING], r.count(b, job) - 1)
                        for t in range(T):
                            last = turn(r, job, t * P, rz1[:, t, m * P:(m + 1) * P])
                        last.then_inc(r.full[job % RING], 1)
                        yield
                else:
                    pe.wait_ge(recips["b"].sem, recips["b"].at(b, h + 1))
                    job = r.job("zbc", h)
                    pe.wait_ge(r.drained[job % RING], r.count(b, job) - 1)
                    for t in range(T):
                        last = turn(r, job, t * P, RZ["b"][:, h % 2, t:t + 1].broadcast_to([P, P]))
                    last.then_inc(r.full[job % RING], 1)
                    yield

            def scores(h, b):
                m, g = (h - 1) // 4, (h - 1) % 4
                pe.wait_ge(stacked[g].sem, stacked[g].at(b, 64))
                for t in range(T):
                    job = fr.job("scores", h, t)
                    pe.wait_ge(fr.drained[job % RING], fr.count(b, job) - 1)
                    pe.matmul(fr.ps(job)[:, :], stack[0:3 * DH, m, 0, g, t * P:(t + 1) * P],
                                        stack[0:3 * DH, m, 1, g, :], start=True, stop=True).then_inc(fr.full[job % RING], 1)
                    yield

            def project(r, stage, h, b, first, weights, src):
                for m in range(K):
                    job = r.job(stage, h, first + m)
                    pe.wait_ge(r.drained[job % RING], r.count(b, job) - 1)
                    for k in range(K):
                        last = pe.matmul(r.ps(job)[:, :], weights[:, k, m * P:(m + 1) * P], src[:, k, :],
                                         start=k == 0, stop=k == K - 1)
                    last.then_inc(r.full[job % RING], 1)
                    yield

            def project_nodes(r, stage, h, b, weights, src):
                for t in range(T):
                    job = r.job(stage, h, t // 2)
                    if t % 2 == 0:
                        pe.wait_ge(r.drained[job % RING], r.count(b, job) - 1)
                    for k in range(K):
                        last = pe.matmul(r.ps(job)[:, t % 2 * D:(t % 2 + 1) * D], src[:, k, t * P:(t + 1) * P],
                                         weights[:, k, :], start=k == 0, stop=k == K - 1)
                    if t % 2 == 1:
                        last.then_inc(r.full[job % RING], 1)
                        yield

            def steps(half, b):
                for stage, h in STAGES[half] if b is not None else ():
                    if stage == "xpose":
                        yield from xpose(half, h, b)
                    elif stage == "fbc":
                        yield from fbc(half, h, b)
                    elif stage == "wh":
                        yield from wh(half, h, b)
                    elif stage == "ptrans":
                        yield from ptrans(half, h, b)
                    elif stage == "attn":
                        yield from attn(half, h, b)
                    elif stage == "zbc":
                        yield from zbc(half, h, b)
                    elif stage == "scores":
                        yield from scores(h, b)
                    elif stage == "qk":
                        if not later(b):
                            pe.wait_ge(s_w, 16 * (N_LOADS - N_EARLY))
                        for k in range(K):
                            turned = fr.job("xpose", 1, k)
                            pe.wait_ge(fr.drained[turned % RING], fr.count(b, turned))
                        for i, weights in enumerate((WQ, WK)):
                            yield from project(fr, "qk", 1, b, K * i, weights, xtf)
                    elif stage == "v":
                        yield from project_nodes(fr, "v", 1, b, WV, xtf)
                    elif stage == "oproj":
                        pe.wait_ge(o_ready.sem, o_ready.at(b, K))
                        yield from project_nodes(fr, "oproj", 1, b, WO, xtf)
                    elif stage == "w1":
                        for k in range(K):
                            turned = bk.job("xpose", 4, k)
                            pe.wait_ge(bk.drained[turned % RING], bk.count(b, turned))
                        yield from project(bk, "w1", 4, b, 0, FF1, xtb)
                    elif stage == "w2":
                        for k in range(K):
                            hidden = bk.job("w1", 4, k)
                            pe.wait_ge(bk.drained[hidden % RING], bk.count(b, hidden))
                        yield from project_nodes(bk, "w2", 4, b, FF2, ex[:, :].rearrange("p (k n) -> p k n", k=K))

            def program(b_front, b_back):
                take_turns("pe", steps("f", b_front), steps("b", b_back))

            program(0, None)
            program(1, 0)
            with pe.Fori(1, B - 1) as t:
                program(t + 1, t)
            program(None, B - 1)

        @block.scalar
        def _(act):
            act.wait_ge(s_wa, 1)
            act.activation(W0[:, :, O0:], heads_out[0][:, 0:4].rearrange("p (k c) -> p k c", k=K),
                           ACT.Copy).then_inc(s_wa, 1)
            act.activation(W2[:, :, D:], heads_out[0][:, 4:8].rearrange("p (k c) -> p k c", k=K),
                           ACT.Copy).then_inc(s_wa, 1)
            act.activation(W3[:, :, :, D:], heads_out[0][:, 8:24].rearrange("p (k h c) -> p k h c", k=K, h=H3),
                           ACT.Copy).then_inc(s_wa, 1)
            act.activation(W4[:, :, D:], heads_out[0][:, 24:40].rearrange("p (k c) -> p k c", k=H3 * K),
                           ACT.Copy).then_inc(s_wa, 1)

            def copy(dst, src):
                return act.activation(dst, src, ACT.Copy)

            def exp(half, h, b):
                z = zbuf(half, h)
                for t in range(T):
                    if additive(half, h):
                        act.wait_ge(logits[half].sem, logits[half].at(b, logit_steps(half, h) + 3 + t))
                    elif t == 0:
                        act.wait_ge(logits[half].sem, logits[half].at(b, logit_steps(half, h) + 1))
                    total = ZS[half][:, h % 2, t:t + 1] if additive(half, h) else zs1[:, t, h - 1:h]
                    act.activation(z[:, t, :], z[:, t, :], ACT.Exp, bias=NM[half][:, h % 2, t:t + 1],
                                   scale=1.0 if additive(half, h) else SCALE,
                                   accum_out=total).then_inc(probs[half].sem, 1)
                    yield

            def evacuate(r, b, job, dst, src):
                act.wait_ge(r.full[job % RING], r.count(b, job))
                copy(dst, src).then_inc(r.drained[job % RING], 1)
                yield

            def steps(half, b):
                for stage, h in STAGES[half] if b is not None else ():
                    r = ring[half]
                    if stage == "exp":
                        yield from exp(half, h, b)
                    elif stage == "xpose":
                        job = r.job("xpose", h, 0)
                        yield from evacuate(r, b, job, (xtf if half == "f" else xtb)[:, 0, :], r.ps(job)[:, :])
                    elif stage == "wh":
                        whs, n = projected(half, h)
                        for k in range(0, banks(half, "wh", h), 2):
                            job, per = r.job("wh", h, k), T // banks(half, "wh", h)
                            yield from evacuate(r, b, job, whs[:, per * k:per * (k + 1), :],
                                                r.ps(job)[:, 0:per * (n + 2)].rearrange("p (t n) -> p t n", t=per))
                    elif stage == "ptrans":
                        for t in range(T):
                            if turned_by_vector(half, h, t):
                                continue
                            if (half, h, t) == ("f", 1, 0):
                                for g in range(4):
                                    act.wait_ge(stacked[g].sem, stacked[g].at(b, 64))
                            job = r.job("ptrans", h, t)
                            yield from evacuate(r, b, job, pt(half, h)[:, :, t * P:(t + 1) * P],
                                     r.ps(job)[:, :].rearrange("p (j i) -> p j i", j=T))
                    elif stage == "qk":
                        if not later(b):
                            act.wait_ge(s_w, 16 * (N_LOADS - N_EARLY))
                        for n in range(2 * K):
                            i, m = divmod(n, K)
                            job = r.job("qk", 1, n)
                            act.wait_ge(r.full[job % RING], r.count(b, job))
                            act.activation(parts[:, m, 1 + i, :].bitcast(F32R), r.ps(job)[:, :], ACT.Identity,
                                           bias=BQK[:, i, m:m + 1]).then_inc(high_part.sem, 1)
                            yield
                    elif (half, stage) == ("f", "zbc"):
                        act.wait_ge(recips["f"].sem, recips["f"].at(b, 2))
                        copy(rz1[:, :, :].rearrange("p t (h d) -> p (t h) d", h=H1),
                             rzs[:, :, :].rearrange("p t h -> p (t h)").unsqueeze(2)
                             .broadcast_to([P, T * H1, DH])).then_inc(spread.sem, 1)
                        yield
                        for m in range(K):
                            job = r.job("zbc", 1, m)
                            act.wait_ge(r.full[job % RING], r.count(b, job))
                            copy(rzbf[:, m, :], r.ps(job)[:, :]).then_inc(r.drained[job % RING], 1)
                            yield
                    elif (half, stage) == ("b", "zbc"):
                        job = r.job("zbc", h)
                        act.wait_ge(r.full[job % RING], r.count(b, job))
                        copy(rzbb[:, :], r.ps(job)[:, :]).then_inc(r.drained[job % RING], 1)
                        yield
                    elif (half, stage) == ("b", "attn"):
                        for k in range(K):
                            output = r.job("attn", h, k)
                            act.wait_ge(r.drained[output % RING], r.count(b, output))
                        act.activation(ex[:, :], pre[:, :], ACT.Exp).then_inc(ex_done.sem, 1)
                        yield
                    elif stage == "w1":
                        for m in range(K):
                            job = r.job("w1", 4, m)
                            act.wait_ge(r.full[job % RING], r.count(b, job))
                            act.activation(ex[:, m * N:(m + 1) * N], r.ps(job)[:, :], ACT.Relu,
                                                   bias=B1[:, m:m + 1]).then_inc(r.drained[job % RING], 1)
                            yield

            def program(b_front, b_back):
                take_turns("act", steps("f", b_front), steps("b", b_back))

            program(0, None)
            program(1, 0)
            with act.Fori(1, B - 1) as t:
                program(t + 1, t)
            program(None, B - 1)

        @block.gpsimd
        def _(pool):
            pool.memset(ident[:, :], 0.0).then_inc(s_id, 1)
            pool.wait_ge(s_id, 1)
            pool.affine_select(out=ident[:, :], in_=ident[:, :], compare_op=ALU.not_equal, fill=1.0,
                               base=0, pattern=[[-1, P]], channel_multiplier=1).then_inc(s_id, 1)
            pool.memset(minus_half[:, :], -0.5).then_inc(s_id, 1)
            pool.wait_ge(s_id, 3)
            pool.wait_ge(s_wa, 1)
            pool.wait_ge(s_mask, 1)

            def row(v):
                return v[:, :].unsqueeze(1).broadcast_to([P, T, D])

            def steps(half, b):
                for stage, h in STAGES[half] if b is not None else ():
                    r = ring[half]
                    if stage == "bias":
                        back, before = last_user(half, h)
                        if half == "b" and back:
                            if later(b):
                                pool.wait_ge(normed["b"].sem, normed["b"].at(b, 0))
                        elif not back or later(b):
                            turned = r.job("ptrans", before, T - 1)
                            pool.wait_ge(r.full[turned % RING], r.count(b + back, turned))
                        whs, n = projected(half, h)
                        for t in range(T):
                            node = r.job("wh", h, t * banks(half, "wh", h) // T)
                            pool.wait_ge(r.drained[node % RING], r.count(b, node))
                            pool.tensor_tensor(zbuf(half, h)[:, t, :], mask[:, t, :],
                                               whs[:, t, n:n + 1].broadcast_to([P, N]),
                                               ALU.add).then_inc(biased[half].sem, 1)
                            yield
                    elif stage == "addh":
                        for k in range(2):
                            nodes = r.job("wh", 0, k)
                            pool.wait_ge(r.drained[nodes % RING], r.count(b, nodes))
                        pool.wait_ge(x_loaded.sem, x_loaded.at(b, 16))
                        if later(b):
                            pool.wait_ge(normed["f"].sem, normed["f"].at(b, 0))
                        pool.tensor_tensor(yf[:, :, O0:D], x_in[:, :, O0:D], whf[:, :, 0:O0],
                                           ALU.add).then_inc(added["f"].sem, 1)
                        yield
                    elif stage == "xbo":
                        if not later(b):
                            pool.wait_ge(s_w, 16 * (N_LOADS - N_EARLY))
                        pool.wait_ge(normed["f"].sem, normed["f"].at(b, T))
                        pool.tensor_tensor(yf[:, :, :], xf[:, :, :], row(BO), ALU.add).then_inc(added["f"].sem, 1)
                        yield
                    elif stage == "xbeta":
                        pool.wait_ge(normed["f"].sem, normed["f"].at(b, 3 * T))
                        if later(b):
                            pool.wait_ge(normed["b"].sem, normed["b"].at(b, 0))
                        pool.tensor_tensor(xb[:, :, :], xf[:, :, :], row(BETA), ALU.add).then_inc(added["b"].sem, 1)
                        yield
                    elif stage == "w2":
                        pool.wait_ge(elu_done.sem, elu_done.at(b, B_HEADS))
                        pool.tensor_tensor(yb[:, :, :], ob[:, :, :], row(B2), ALU.add).then_inc(added["b"].sem, 1)
                        yield
                    elif stage == "norm":
                        n = h if half == "f" else h - 3
                        pool.wait_ge(stats[half].sem, stats[half].at(b, stat_steps(half, n) + 3))
                        pool.tensor_tensor(RS[half][:, :], VE[half][:, :], minus_half[:, :],
                                           ALU.pow).then_inc(rstd[half].sem, 1)
                        yield

            def program(b_front, b_back):
                take_turns("pool", steps("f", b_front), steps("b", b_back))

            program(0, None)
            program(1, 0)
            with pool.Fori(1, B - 1) as t:
                program(t + 1, t)
            program(None, B - 1)

        @block.vector
        def _(dve):
            dve.wait_ge(s_adj, 16)
            zb = Z["b"][:, :, :, :].rearrange("p a t n -> p (a t n)")
            dve.tensor_scalar(mask[:, :, :].rearrange("p t n -> p (t n)"), zb[:, 0:T * N].bitcast(I32), FAR, -FAR,
                              ALU.mult, ALU.add).then_inc(s_mask, 1)
            dve.wait_ge(s_mask, 1)
            dve.wait_ge(s_wa, 5)

            def evacuate(r, b, job, dst, src):
                dve.wait_ge(r.full[job % RING], r.count(b, job))
                dve.tensor_copy(dst, src).then_inc(r.drained[job % RING], 1)
                yield

            def maxima(half, h, b):
                r = ring[half]
                z, g, ng, nm = zbuf(half, h), G[half][:, h % 2], NG[half][:, h % 2], NM[half][:, h % 2]
                step = logit_steps(half, h)
                if additive(half, h):
                    job = r.job("fbc", h)
                    seen = ahead(dve, r.count(b, job))
                    dve.wait_ge(s_adj, 16)
                    dve.wait_ge(r.full[job % RING], seen)
                    for t in range(T):
                        index = (0 if h == 0 else 1) if half == "f" else h
                        seen = ahead(dve, biased[half].at(b, T * index + t + 1))
                        dve.wait_ge(s_adj, 16)
                        dve.wait_ge(biased[half].sem, seen)
                        last = dve.tensor_tensor_reduce(z[:, t, :], r.ps(job)[:, :], z[:, t, :], 1.0, -3e38,
                                                        ALU.add, ALU.max, g[:, t:t + 1])
                        if t < T - 1:
                            yield
                    last.then_inc(r.drained[job % RING], 1)
                    yield
                    dve.wait_ge(r.drained[job % RING], r.count(b, job))
                    dve.tensor_scalar(ng, g, -1.0, None, ALU.mult).then_inc(logits[half].sem, 1)
                    yield
                    dve.wait_ge(logits[half].sem, logits[half].at(b, step + 1))
                    dve.scalar_tensor_tensor(out=nm, in0=ng, scalar=slope(half, h), in1=ng,
                                             op0=ALU.mult, op1=ALU.min).then_inc(logits[half].sem, 1)
                    yield
                    for t in range(T):
                        dve.scalar_tensor_tensor(out=z[:, t, :], in0=z[:, t, :], scalar=slope(half, h), in1=z[:, t, :],
                                                 op0=ALU.mult, op1=ALU.max).then_inc(logits[half].sem, 1)
                        yield
                else:
                    for t in range(T):
                        job = r.job("scores", h, t)
                        seen = ahead(dve, r.count(b, job))
                        dve.wait_ge(s_adj, 16)
                        dve.wait_ge(r.full[job % RING], seen)
                        dve.tensor_tensor_reduce(z[:, t, :], r.ps(job)[:, :], mask[:, t, :], 1.0, -3e38,
                                                         ALU.add, ALU.max, g[:, t:t + 1]).then_inc(r.drained[job % RING], 1)
                        yield
                    dve.wait_ge(r.drained[job % RING], r.count(b, job))
                    dve.tensor_scalar(nm, g, -SCALE, None, ALU.mult).then_inc(logits[half].sem, 1)
                    yield

            def recip(half, h, b):
                dve.wait_ge(probs[half].sem, probs[half].at(b, T * h + T))
                if (half, h) == ("f", H1):
                    dve.reciprocal(rzs[:, :, :], zs1[:, :, :]).then_inc(recips["f"].sem, 1)
                    yield
                else:
                    dve.reciprocal(RZ[half][:, h % 2, :], ZS[half][:, h % 2, :]).then_inc(recips[half].sem, 1)
                    yield

            def elu(h, b, dst):
                dve.wait_ge(ex_done.sem, ex_done.at(b, h + 1))
                dve.tensor_scalar(ex[:, :], ex[:, :], 1.0, -1.0, ALU.min, ALU.add).then_inc(elu_low.sem, 1)
                yield
                dve.wait_ge(elu_low.sem, elu_low.at(b, h + 1))
                dve.tensor_tensor(dst, pre[:, :], ex[:, :], ALU.max).then_inc(elu_done.sem, 1)
                yield

            def attn(half, h, b):
                r = ring[half]
                if half == "f" and not additive(half, h):
                    return
                rz = RZ[half][:, h % 2]
                if half == "f":
                    dve.wait_ge(recips["f"].sem, recips["f"].at(b, 1 if h == 0 else 3))
                    n = O0 if h == 0 else D
                    per = BANK // n
                    src = x_in if h == 0 else xf
                    for t in range(T):
                        job = r.job("attn", h, t // per)
                        if t % per == 0:
                            dve.wait_ge(r.full[job % RING], r.count(b, job))
                        last = dve.scalar_tensor_tensor(out=yf[:, t, 0:n], in0=r.ps(job)[:, t % per * n:(t % per + 1) * n],
                                                        scalar=rz[:, t:t + 1], in1=src[:, t, 0:n],
                                                        op0=ALU.mult, op1=ALU.add)
                        if t % per == per - 1:
                            last.then_inc(r.drained[job % RING], 1)
                            yield
                elif h < H3:
                    turned = r.job("zbc", h)
                    dve.wait_ge(r.drained[turned % RING], r.count(b, turned))
                    for k in range(K):
                        job = r.job("attn", h, k)
                        dve.wait_ge(r.full[job % RING], r.count(b, job))
                        dve.tensor_tensor(pre[:, k * N:(k + 1) * N], r.ps(job)[:, :], rzbb[:, :], ALU.mult).then_inc(r.drained[job % RING], 1)
                        yield
                    yield from elu(h, b, ht[:, K * h:K * (h + 1), :].rearrange("p k n -> p (k n)"))
                else:
                    dve.wait_ge(recips["b"].sem, recips["b"].at(b, B_HEADS))
                    for t in range(T):
                        job = r.job("attn", h, t // 2)
                        if t % 2 == 0:
                            dve.wait_ge(r.full[job % RING], r.count(b, job))
                        last = dve.tensor_scalar(pre[:, t * D:(t + 1) * D], r.ps(job)[:, t % 2 * D:(t % 2 + 1) * D],
                                                 rz[:, t:t + 1], None, ALU.mult)
                        if t % 2 == 1:
                            last.then_inc(r.drained[job % RING], 1)
                            yield
                    if later(b):
                        dve.wait_ge(stored.sem, stored.at(b, 0))
                    yield from elu(h, b, ob[:, :, :].rearrange("p t d -> p (t d)"))

            def norm(half, n, y, dst, b):
                for t in range(T):
                    last = dve.bn_stats(ST[half][:, t, :], y[:, t, :])
                last.then_inc(stats[half].sem, 1)
                yield
                seen = ahead(dve, stats[half].at(b, stat_steps(half, n) + 1))
                dve.wait_ge(s_adj, 16)
                dve.wait_ge(stats[half].sem, seen)
                for t in range(T):
                    last = dve.bn_aggr(MV[half][:, t, :], ST[half][:, t, :])
                last.then_inc(stats[half].sem, 1)
                yield
                dve.wait_ge(stats[half].sem, stats[half].at(b, stat_steps(half, n) + 2))
                dve.tensor_scalar(VE[half][:, :], MV[half][:, :, 1], EPS, None, ALU.add).then_inc(stats[half].sem, 1)
                yield
                if (half, n) == ("b", 0):
                    for t in range(T):
                        last = dve.scalar_tensor_tensor(out=dst[:, t, :], in0=y[:, t, :], scalar=MV[half][:, t, 0:1],
                                                        in1=GAMMA[:, :], op0=ALU.subtract, op1=ALU.mult)
                    last.then_inc(stats[half].sem, 1)
                    yield
                    dve.wait_ge(stats[half].sem, stats[half].at(b, 4))
                    dve.wait_ge(rstd[half].sem, rstd[half].at(b, n + 1))
                    for t in range(T):
                        dve.scalar_tensor_tensor(out=y[:, t, :], in0=dst[:, t, :], scalar=RS[half][:, t:t + 1],
                                                 in1=xb[:, t, :], op0=ALU.mult,
                                                 op1=ALU.add).then_inc(normed[half].sem, 1)
                        yield
                    return
                dve.wait_ge(rstd[half].sem, rstd[half].at(b, n + 1))
                for t in range(T):
                    dve.tensor_scalar(dst[:, t, :], y[:, t, :], MV[half][:, t, 0:1], RS[half][:, t:t + 1],
                                      ALU.subtract, ALU.mult).then_inc(normed[half].sem, 1)
                    yield

            def steps(half, b):
                for stage, h in STAGES[half] if b is not None else ():
                    r = ring[half]
                    if stage == "fbc" or stage == "scores":
                        yield from maxima(half, h, b)
                    elif stage == "xpose":
                        job = r.job("xpose", h, 1)
                        yield from evacuate(r, b, job, (xtf if half == "f" else xtb)[:, 1, :], r.ps(job)[:, :])
                    elif stage == "wh":
                        whs, n = projected(half, h)
                        for k in range(1, banks(half, "wh", h), 2):
                            job, per = r.job("wh", h, k), T // banks(half, "wh", h)
                            yield from evacuate(r, b, job, whs[:, per * k:per * (k + 1), :],
                                                r.ps(job)[:, 0:per * (n + 2)].rearrange("p (t n) -> p t n", t=per))
                    elif stage == "ptrans":
                        for t in range(T):
                            if not turned_by_vector(half, h, t):
                                continue
                            if (half, h, t) == ("f", 1, 1):
                                for g in range(4):
                                    dve.wait_ge(stacked[g].sem, stacked[g].at(b, 64))
                            if t == T - 1 and (additive(half, h) or h == H1):
                                yield from recip(half, h, b)
                            job = r.job("ptrans", h, t)
                            yield from evacuate(r, b, job, pt(half, h)[:, :, t * P:(t + 1) * P],
                                     r.ps(job)[:, :].rearrange("p (j i) -> p j i", j=T))
                    elif stage == "attn":
                        yield from attn(half, h, b)
                    elif stage == "qk":
                        if not later(b):
                            dve.wait_ge(s_w, 16 * (N_LOADS - N_EARLY))
                        for n in range(2 * K):
                            i, m = divmod(n, K)
                            job = r.job("qk", 1, n)
                            dve.wait_ge(high_part.sem, high_part.at(b, n + 1))
                            dve.scalar_tensor_tensor(
                                out=parts[:, m, 3 * i, :].bitcast(F32R), in0=r.ps(job)[:, :],
                                scalar=BQK[:, i, m:m + 1], in1=parts[:, m, 1 + i, :],
                                op0=ALU.add, op1=ALU.subtract).then_inc(r.drained[job % RING], 1)
                            yield
                    elif stage == "v":
                        for n in range(2):
                            job = r.job("v", 1, n)
                            dve.wait_ge(r.full[job % RING], r.count(b, job))
                            dve.tensor_tensor(whf[:, 2 * n:2 * n + 2, 0:D],
                                                      r.ps(job)[:, :].rearrange("p (t n) -> p t n", t=2),
                                                      BV[:, :].unsqueeze(1).broadcast_to([P, 2, D]), ALU.add).then_inc(r.drained[job % RING], 1)
                            yield
                    elif (half, stage) == ("f", "zbc"):
                        dve.wait_ge(heads_done.sem, heads_done.at(b, H1))
                        for m in range(K):
                            turned = r.job("zbc", 1, m)
                            dve.wait_ge(r.drained[turned % RING], r.count(b, turned))
                        for m in range(K):
                            dve.tensor_tensor(xtf[:, m, :], heads_out[m][:, :], rzbf[:, m, :],
                                              ALU.mult).then_inc(o_ready.sem, 1)
                            yield
                    elif stage == "oproj" or stage == "w2":
                        y = yf if stage == "oproj" else yb
                        dve.wait_ge(added[half].sem, added[half].at(b, 2))
                        for n in range(2):
                            job = r.job(stage, h, n)
                            dve.wait_ge(r.full[job % RING], r.count(b, job))
                            dve.tensor_tensor(y[:, 2 * n:2 * n + 2, :],
                                                      r.ps(job)[:, :].rearrange("p (t n) -> p t n", t=2),
                                                      y[:, 2 * n:2 * n + 2, :], ALU.add).then_inc(r.drained[job % RING], 1)
                            yield
                    elif (half, stage) == ("f", "norm"):
                        for job in {0: [r.job("attn", 0)], 1: [r.job("oproj", 1, k) for k in range(2)],
                                    2: [r.job("attn", 9, k) for k in range(2)]}[h]:
                            dve.wait_ge(r.drained[job % RING], r.count(b, job))
                        if h == 0:
                            dve.wait_ge(added["f"].sem, added["f"].at(b, 1))
                            if later(b):
                                dve.wait_ge(added["b"].sem, added["b"].at(b - 1, 1))
                                turned = bk.job("xpose", 0, K - 1)
                                dve.wait_ge(bk.full[turned % RING], bk.count(b - 1, turned))
                        yield from norm("f", h, yf, xf, b)
                    elif (half, stage, h) == ("b", "norm", 3):
                        for k in range(2):
                            job = r.job("w2", 4, k)
                            dve.wait_ge(r.drained[job % RING], r.count(b, job))
                        yield from norm("b", 0, yb, ob, b)
                    elif (half, stage, h) == ("b", "norm", 4):
                        dve.wait_ge(normed["b"].sem, normed["b"].at(b, T))
                        yield from norm("b", 1, yb, ob, b)

            def program(b_front, b_back):
                take_turns("dve", steps("f", b_front), steps("b", b_back))

            program(0, None)
            program(1, 0)
            with dve.Fori(1, B - 1) as t:
                program(t + 1, t)
            program(None, B - 1)


N_LOADS, N_EARLY = 25, 9


def kernel(**inputs):
    import numpy as np
    import concourse.bacc as bacc
    from concourse.bass_utils import run_bass_kernel_spmd as run

    a = {k: np.asarray(v) for k, v in inputs.items()}

    def tiles(m):
        return m.reshape(m.shape[0] // P, P, *m.shape[1:]).swapaxes(0, 1)

    def rows(v):
        return np.broadcast_to(v, (P, v.shape[0]))

    h0, w3, a3 = a["L0_gnn_a"], a["L3_gnn_W_heads"], a["L3_gnn_a_heads"]
    data = {
        "x": a["x"].reshape(B, T, P, D).swapaxes(1, 2), "adj": tiles(a["adj"]).reshape(P, T * N),
        "w0": tiles(a["L0_gnn_W"]), "w0t": a["L0_gnn_W"].T, "a0": h0[:, :, 0].T,
        "wq": tiles(a["L1_gnn_Wq"].T), "wk": tiles(a["L1_gnn_Wk"].T), "wv": tiles(a["L1_gnn_Wv"].T),
        "wo": tiles(a["L1_gnn_Wo"].T),
        "bqk": np.stack([tiles(a["L1_gnn_bq"]), tiles(a["L1_gnn_bk"])], 1),
        "bv": rows(a["L1_gnn_bv"]), "bo": rows(a["L1_gnn_bo"]),
        "w2": tiles(a["L2_gnn_W"]), "w2t": tiles(a["L2_gnn_W"].T).reshape(P, K * D),
        "a2": tiles(np.stack([a["L2_gnn_a_src"], a["L2_gnn_a_dst"]], 1)),
        "w3": tiles(w3.transpose(1, 0, 2)),
        "w3t": w3.transpose(0, 2, 1).reshape(H3, K, P, D).transpose(2, 0, 1, 3).reshape(P, H3 * K * D),
        "a3": tiles(a3.reshape(H3, 2, D).transpose(2, 0, 1)),
        "w4": tiles(a["L3_gnn_W_out"]), "w4t": tiles(a["L3_gnn_W_out"].T).reshape(P, K * H3 * D),
        "a4": tiles(a["L3_gnn_a_out"].reshape(2, D).T),
        "f1": tiles(a["L3_gnn_w1"]), "b1": tiles(a["L3_gnn_b1"]), "f2": tiles(a["L3_gnn_w2"]),
        "b2": rows(a["L3_gnn_b2"]), "gamma": rows(a["L3_gnn_ln_gamma"]), "beta": rows(a["L3_gnn_ln_beta"]),
    }
    data = {k: np.ascontiguousarray(v) for k, v in data.items()}
    nc = bacc.Bacc("TRN2", target_bir_lowering=False, num_devices=1)
    dram = {k: nc.dram_tensor(k + "_dram", v.shape, mybir.dt.from_np(v.dtype), kind="ExternalInput").ap()
            for k, v in data.items()}
    out = nc.dram_tensor("out_dram", (B, P, T, D), F32, kind="ExternalOutput").ap()
    graph_layers(nc, dram.pop("x"), dram.pop("adj"), dram, out)
    r = run(nc, [{k + "_dram": v for k, v in data.items()}], core_ids=[0])
    got = r.results[0]["out_dram"]
    return np.ascontiguousarray(got.swapaxes(1, 2)).reshape(B, N, D)
```
